# Optimizing a Trainium2 kernel written in Bass

```python
import numpy as np
import jax
import jax.numpy as jnp

def _softmax(x, axis=-1):
    return jax.nn.softmax(x, axis=axis)

def _gelu(x):
    return jax.nn.gelu(x, approximate=True)

def _silu(x):
    return jax.nn.silu(x)

def _sigmoid(x):
    return jax.nn.sigmoid(x)

def _layernorm(x, axis=-1, eps=1e-05):
    m = jnp.mean(x, axis=axis, keepdims=True)
    v = jnp.var(x, axis=axis, keepdims=True)
    return (x - m) / jnp.sqrt(v + eps)

def _scatter_add(tgt, idx, src, axis=0):
    return tgt.at[idx].add(src)

def _segment_sum(src, seg, n):
    return jax.ops.segment_sum(src, seg, n)
kernel_name = 'mk_seq_postln_d2_jaxref_r8_3eb1c5'

def setup_inputs(seed: int=0):
    np.random.seed(seed)
    _w = jnp.asarray

    def _L0_attn_setup():
        import jax, jax.numpy as jnp
        import numpy as np
        EPS = 1e-06

        def _rmsnorm(x, scale):
            var = jnp.mean(jnp.square(x), axis=-1, keepdims=True)
            return x * jax.lax.rsqrt(var + EPS) * scale
        key = jax.random.key(seed)
        ks = jax.random.split(key, 6)
        B, S, D, H, Dh = (2, 256, 128, 16, 64)
        x = jax.random.normal(ks[0], (B, S, D), dtype=jnp.float32)
        norm_scale = jnp.ones((D,), dtype=jnp.float32)
        wq = jax.random.normal(ks[1], (D, H, Dh), dtype=jnp.float32) / np.sqrt(D)
        wk = jax.random.normal(ks[2], (D, H, Dh), dtype=jnp.float32) / np.sqrt(D)
        wv = jax.random.normal(ks[3], (D, H, Dh), dtype=jnp.float32) / np.sqrt(D)
        w_out = jax.random.normal(ks[4], (H, Dh, D), dtype=jnp.float32) / np.sqrt(H * Dh)
        b_out = jnp.zeros((D,), dtype=jnp.float32)
        return {'x': x, 'norm_scale': norm_scale, 'wq': wq, 'wk': wk, 'wv': wv, 'w_out': w_out, 'b_out': b_out}
    _L0_attn_in = _L0_attn_setup()

    def _L0_ffn_setup():
        import jax, jax.numpy as jnp
        import numpy as np
        D = 128
        H = 256
        E = 8
        TOP_K = 2
        N_SHARED = 1
        B, S = (2, 128)
        key = jax.random.key(seed)
        ks = jax.random.split(key, 12)
        sc = 0.02
        return {'hidden': jax.random.normal(ks[0], (B, S, D), jnp.float32), 'router_w': jax.random.normal(ks[1], (D, E), jnp.float32) * sc, 'router_b': jnp.zeros((E,), jnp.float32), 'sw1': jax.random.normal(ks[2], (D, H), jnp.float32) * sc, 'sb1': jnp.zeros((H,), jnp.float32), 'sw2': jax.random.normal(ks[3], (H, D), jnp.float32) * sc, 'sb2': jnp.zeros((D,), jnp.float32), 'rw1': jax.random.normal(ks[4], (E, D, H), jnp.float32) * sc, 'rb1': jnp.zeros((E, H), jnp.float32), 'rw2': jax.random.normal(ks[5], (E, H, D), jnp.float32) * sc, 'rb2': jnp.zeros((E, D), jnp.float32)}
    _L0_ffn_in = _L0_ffn_setup()

    def _L1_attn_setup():
        import jax, jax.numpy as jnp
        import numpy as np
        N_HEADS = 16
        SCALE = 8.0
        key = jax.random.key(seed)
        k1, k2, k3, k4 = jax.random.split(key, 4)
        b, n, d_model, inner = (8, 256, 128, 128)
        x = jax.random.normal(k1, (b, n, d_model), dtype=jnp.float32)
        Wqkv = jax.random.normal(k2, (3 * inner, d_model), dtype=jnp.float32) * (1.0 / np.sqrt(d_model))
        Wproj = jax.random.normal(k3, (d_model, inner), dtype=jnp.float32) * (1.0 / np.sqrt(inner))
        bproj = jax.random.normal(k4, (d_model,), dtype=jnp.float32) * 0.01
        return {'x': x, 'Wqkv': Wqkv, 'Wproj': Wproj, 'bproj': bproj}
    _L1_attn_in = _L1_attn_setup()

    def _L1_ffn_setup():
        import jax, jax.numpy as jnp
        import numpy as np
        B, S, D, E, K = (4, 256, 128, 8, 2)
        H = 4 * D
        key = jax.random.key(seed)
        k0, k1, k2, k3 = jax.random.split(key, 4)
        x = jax.random.normal(k0, (B, S, D), dtype=jnp.float32)
        router_w = jax.random.normal(k1, (E, D), dtype=jnp.float32) * 0.02
        w1 = jax.random.normal(k2, (E, H, D), dtype=jnp.float32) * 0.02
        w2 = jax.random.normal(k3, (E, D, H), dtype=jnp.float32) * 0.02
        return {'x': x, 'router_w': router_w, 'w1': w1, 'w2': w2}
    _L1_ffn_in = _L1_ffn_setup()
    _d = {'L0_attn_x': _L0_attn_in['x'], 'L0_attn_norm_scale': _L0_attn_in['norm_scale'], 'L0_attn_wq': _L0_attn_in['wq'], 'L0_attn_wk': _L0_attn_in['wk'], 'L0_attn_wv': _L0_attn_in['wv'], 'L0_attn_w_out': _L0_attn_in['w_out'], 'L0_attn_b_out': _L0_attn_in['b_out'], 'L0_ffn_router_w': _L0_ffn_in['router_w'], 'L0_ffn_router_b': _L0_ffn_in['router_b'], 'L0_ffn_sw1': _L0_ffn_in['sw1'], 'L0_ffn_sb1': _L0_ffn_in['sb1'], 'L0_ffn_sw2': _L0_ffn_in['sw2'], 'L0_ffn_sb2': _L0_ffn_in['sb2'], 'L0_ffn_rw1': _L0_ffn_in['rw1'], 'L0_ffn_rb1': _L0_ffn_in['rb1'], 'L0_ffn_rw2': _L0_ffn_in['rw2'], 'L0_ffn_rb2': _L0_ffn_in['rb2'], 'L1_attn_Wqkv': _L1_attn_in['Wqkv'], 'L1_attn_Wproj': _L1_attn_in['Wproj'], 'L1_attn_bproj': _L1_attn_in['bproj'], 'L1_ffn_router_w': _L1_ffn_in['router_w'], 'L1_ffn_w1': _L1_ffn_in['w1'], 'L1_ffn_w2': _L1_ffn_in['w2']}
    _x0 = _d['L0_attn_x']
    _d['L0_attn_x'] = jax.random.normal(jax.random.fold_in(jax.random.key(seed), 1), (16, 256, 128), dtype=_x0.dtype)
    del _x0
    return _d

def reference(L0_attn_x, L0_attn_norm_scale, L0_attn_wq, L0_attn_wk, L0_attn_wv, L0_attn_w_out, L0_attn_b_out, L0_ffn_router_w, L0_ffn_router_b, L0_ffn_sw1, L0_ffn_sb1, L0_ffn_sw2, L0_ffn_sb2, L0_ffn_rw1, L0_ffn_rb1, L0_ffn_rw2, L0_ffn_rb2, L1_attn_Wqkv, L1_attn_Wproj, L1_attn_bproj, L1_ffn_router_w, L1_ffn_w1, L1_ffn_w2):

    def _L0_attn_ref(x, norm_scale, wq, wk, wv, w_out, b_out):
        import jax, jax.numpy as jnp
        import numpy as np
        EPS = 1e-06

        def _rmsnorm(x, scale):
            var = jnp.mean(jnp.square(x), axis=-1, keepdims=True)
            return x * jax.lax.rsqrt(var + EPS) * scale
        dtype = x.dtype
        softmax_dtype = jnp.float32
        h = _rmsnorm(x, norm_scale)
        q = jnp.einsum('bsd,dhe->bshe', h, wq)
        k = jnp.einsum('bsd,dhe->bshe', h, wk)
        v = jnp.einsum('bsd,dhe->bshe', h, wv)
        head_dim = q.shape[-1]
        scale = head_dim ** (-0.5)
        q = (q * scale).astype(softmax_dtype)
        kf = k.astype(softmax_dtype)
        weights = jnp.einsum('bqhd,bkhd->bhqk', q, kf)
        weights = jax.nn.softmax(weights, axis=-1).astype(dtype)
        new_vals = jnp.einsum('bhqk,bkhd->bqhd', weights, v).astype(dtype)
        out = jnp.einsum('bqhe,hed->bqd', new_vals, w_out) + b_out
        return out

    def _L0_ffn_ref(hidden, router_w, router_b, sw1, sb1, sw2, sb2, rw1, rb1, rw2, rb2):
        import jax, jax.numpy as jnp
        import numpy as np
        D = 128
        H = 256
        E = 8
        TOP_K = 2
        N_SHARED = 1
        B, S = (2, 128)
        b, s, d = hidden.shape
        T = b * s
        flat = hidden.reshape(T, d)
        router_logits = flat @ router_w + router_b
        router_probs = jax.nn.softmax(router_logits, axis=-1)
        topk_probs, topk_idx = jax.lax.top_k(router_probs, TOP_K)
        weights = jnp.zeros_like(router_probs).at[jnp.arange(T)[:, None], topk_idx].add(topk_probs)
        sh = jax.nn.gelu(flat @ sw1 + sb1, approximate=False)
        shared_out = (sh @ sw2 + sb2) / N_SHARED
        h1 = jax.nn.gelu(jnp.einsum('td,edh->teh', flat, rw1) + rb1[None], approximate=False)
        expert_out = jnp.einsum('teh,ehd->ted', h1, rw2) + rb2[None]
        mixed = jnp.einsum('ted,te->td', expert_out, weights)
        return (shared_out + mixed).reshape(b, s, d)

    def _L1_attn_ref(x, Wqkv, Wproj, bproj):
        import jax, jax.numpy as jnp
        import numpy as np
        N_HEADS = 16
        SCALE = 8.0
        b, n, _ = x.shape
        qkv = jnp.einsum('bnm,fm->bnf', x, Wqkv)
        qkv = qkv.reshape(b, n, N_HEADS, -1)
        dh = qkv.shape[3] // 3
        q, k, v = (qkv[..., :dh], qkv[..., dh:2 * dh], qkv[..., 2 * dh:])
        scores = jnp.einsum('bnhd,bngd->bnhg', q, k) / SCALE
        attn = jax.nn.softmax(scores, axis=-1)
        out = jnp.einsum('bnhg,bngd->bnhd', attn, v)
        out = out.reshape(b, n, -1)
        return jnp.einsum('bni,mi->bnm', out, Wproj) + bproj

    def _L1_ffn_ref(x, router_w, w1, w2):
        import jax, jax.numpy as jnp
        import numpy as np
        B, S, D, E, K = (4, 256, 128, 8, 2)
        H = 4 * D
        b, s, d = x.shape
        e = router_w.shape[0]
        logits = jnp.einsum('bsd,ed->bse', x, router_w)
        probs = jax.nn.softmax(logits, axis=-1)
        topk_vals, topk_idx = jax.lax.top_k(probs, K)
        x_flat = x.reshape(b * s, d)
        vals = topk_vals.reshape(b * s, K)
        idx = topk_idx.reshape(b * s, K)
        out = jnp.zeros_like(x_flat)
        for eid in range(e):
            w = jnp.sum(jnp.where(idx == eid, vals, jnp.zeros((), x.dtype)), axis=-1)
            h = jax.nn.gelu(x_flat @ w1[eid].T, approximate=False)
            y = h @ w2[eid].T
            out = out + w[:, None] * y
        return out.reshape(b, s, d)
    x = L0_attn_x
    x = _layernorm(x + _L0_attn_ref(x, L0_attn_norm_scale, L0_attn_wq, L0_attn_wk, L0_attn_wv, L0_attn_w_out, L0_attn_b_out), axis=-1)
    x = _layernorm(x + _L0_ffn_ref(x, L0_ffn_router_w, L0_ffn_router_b, L0_ffn_sw1, L0_ffn_sb1, L0_ffn_sw2, L0_ffn_sb2, L0_ffn_rw1, L0_ffn_rb1, L0_ffn_rw2, L0_ffn_rb2), axis=-1)
    x = _layernorm(x + _L1_attn_ref(x, L1_attn_Wqkv, L1_attn_Wproj, L1_attn_bproj), axis=-1)
    x = _layernorm(x + _L1_ffn_ref(x, L1_ffn_router_w, L1_ffn_w1, L1_ffn_w2), axis=-1)
    return x

_drawn_inputs = setup_inputs


def setup_inputs(seed=0):
    import zlib

    import numpy as np

    out = dict(_drawn_inputs(seed))
    spreads = {'L0_attn_norm_scale': (1.0, 0.2),
     'L0_attn_b_out': (0.0, 0.1),
     'L0_ffn_router_b': (0.0, 0.631),
     'L0_ffn_sb1': (0.0, 0.51),
     'L0_ffn_sb2': (0.0, 0.1),
     'L0_ffn_rb1': (0.0, 0.8),
     'L0_ffn_rb2': (0.0, 0.34)}
    factors = {'L0_ffn_rw1': 6.506,
     'L0_ffn_rw2': 5.839,
     'L1_attn_bproj': 5.695,
     'L1_ffn_router_w': 5.284,
     'L1_ffn_w1': 4.695,
     'L1_ffn_w2': 4.652}
    for name, (base, spread) in spreads.items():
        noise = np.random.default_rng([zlib.crc32(name.encode()), seed]).standard_normal(out[name].shape)
        drawn = base * np.exp(spread * noise) if base else spread * noise
        out[name] = jnp.asarray(drawn.astype(out[name].dtype))
    for name, factor in factors.items():
        out[name] = (out[name] * factor).astype(out[name].dtype)
    return out
```

```python
import concourse.bass as bass
from concourse import mybir
from contextlib import ExitStack

F32 = mybir.dt.float32
ALU = mybir.AluOpType
ACT = mybir.ActivationFunctionType
AX = mybir.AxisListType

P = 128
ROWS, S, D = 16, 256, 128
NT = S // P
H, DH = 16, 64
HP = H // 2
E = 8
HID0, HID1 = 256, 512
M0, M1 = HID0 // P, HID1 // P
NH1, DH1 = 16, 8
LN_EPS, RMS_EPS = 1e-5, 1e-6
FIRST, LAST = 2, ROWS - 2



def slot_fill(it, s):
    b, c = 1 <= it <= ROWS, 2 <= it <= ROWS + 1
    out = []
    if b:
        out += {0: ["D0base", "D0p0", "D0p1"], 1: ["D0p2", "D0p3"], 2: ["X2T"], 3: ["LQ0", "LQ1"],
                6: [], 7: ["AOT", "PROJ"]}.get(s, [])
    if c:
        out += {3: ["D1p0"], 4: ["D1p1"], 5: ["D1p2"], 6: ["D1p3"]}.get(s, [])
    return out


def pe_units(it):
    a, b, c, nxt = it < ROWS, 1 <= it <= ROWS, 2 <= it <= ROWS + 1, it < ROWS - 1
    order = []
    turn = {"A": 0, "F": 0, "G": 0}

    def put(name, ring):
        banks = {"A": ["A0", "A1"], "F": ["F0", "F1"], "G": ["F0", "F1", "T0", "T1"]}.get(ring, [ring])
        order.append((name, banks[turn.get(ring, 0) % len(banks)]))
        if ring in turn:
            turn[ring] += 1

    if a:
        for n in ["V0", "V1", "V2", "V3", "QK0", "QK1"]:
            put(n, "A")
        put("S0", "S0")
        put("S1", "S1")
    if b:
        put("WT0", "F")
    for s in range(HP):
        if a:
            put(f"T{2 * s}", "T0")
            put(f"T{2 * s + 1}", "T1")
            if s + 2 < HP:
                put(f"QK{s + 2}", "A")
            if s + 1 < HP:
                put(f"S{2 * s + 2}", "S0")
                put(f"S{2 * s + 3}", "S1")
        for n in slot_fill(it, s):
            put(n, "F")
        if a:
            put(f"O{s}", "A")
            if s:
                put(f"OT{s - 1}", "A")
    if a:
        put(f"OT{HP - 1}", "A")
        put("OUT", "A")
    if b:
        put("X3T", "F")
        put("R1", "F")
        for u in range(8):
            put(f"U1_{u}", "G")
    if a:
        put("X1T", "A")
        put("R0", "A")
    if b:
        for u in range(8, 2 * E):
            put(f"U1_{u}", "G")
    if a:
        for u in range(E + 1):
            put(f"U0_{u}", "G")
    if nxt:
        put("HT", "A")
    return order


PRE = [("HT", "A0")]
BANKS = ["S0", "S1", "T0", "T1", "A0", "A1", "F0", "F1"]


def count_units(it):
    seen = {k: 0 for k in BANKS}
    for units in [PRE] + [pe_units(i) for i in range(it)]:
        for _, bank in units:
            seen[bank] += 1
    return seen


class Iteration:

    def __init__(self, it, step, banks):
        self.it, self.step, self.banks = it, step, banks
        self.a, self.b, self.c = it < ROWS, 1 <= it <= ROWS, 2 <= it <= ROWS + 1
        self.next = it < ROWS - 1
        seen, self.nth = count_units(it), {}
        self.per = {k: 0 for k in BANKS}
        for name, bank in pe_units(it):
            seen[bank] += 1
            self.per[bank] += 1
            self.nth[name] = (bank, seen[bank])

    def at(self, lag, per, k):
        return (self.it - lag) * per + k + self.step * per

    def fill(self, name, before=0):
        bank, n = self.nth[name]
        return self.banks[bank][1], n - before + self.step * self.per[bank]

    def drain(self, name, before=0):
        bank, n = self.nth[name]
        return self.banks[bank][2], n - before + self.step * self.per[bank]

    def bank(self, name):
        return self.banks[self.nth[name][0]][0]


class Before(Iteration):

    def __init__(self, banks):
        self.it, self.step, self.banks = -1, 0, banks
        self.a = self.b = self.c = False
        self.next = True
        self.nth, self.per = {"HT": ("A0", 1)}, {k: 0 for k in BANKS}


def transformer_blocks(nc, x_in, norm_scale, wq_in, wk_in, wv_in, wo_in, b_out_in,
                       router0_in, router0_b_in, sw1_in, sb1_in, sw2_in, sb2_in, rw1_in, rb1_in, rw2_in,
                       rb2_in, wqkv1_in, wproj_in, bproj_in, router1_in, w1_in, w2_in, out):
    ctx = ExitStack()
    with ctx:
        def sb(name, *shape):
            return ctx.enter_context(nc.sbuf_tensor(name, list(shape), F32))

        def sem(name):
            return ctx.enter_context(nc.semaphore(name))

        wq, wk, wv = (sb(n, P, H * DH) for n in ("wq", "wk", "wv"))
        wo = sb("wo", P, HP, D)
        nscale = sb("nscale", P, 1)
        b_out = sb("b_out", P, 1, D)
        bproj = sb("bproj", P, 1, D)
        router0 = sb("router0", P, E)
        router0_b = sb("router0_b", P, 1, E)
        router1 = sb("router1", P, E)
        up0 = sb("up0", P, E + 1, HID0)
        up0_b = sb("up0_b", P, E + 1, M0)
        down0 = sb("down0", P, E + 1, M0, D)
        down0_b = sb("down0_b", E + 1, D)
        wqkv1 = sb("wqkv1", P, 3 * D)
        wproj = sb("wproj", P, D)
        up1 = sb("up1", P, E, HID1)
        down1 = sb("down1", P, E, M1, D)
        ident = sb("ident", P, P)
        minus_half, ln_eps, rms_eps, one_over_d = (sb(n, P, NT) for n in ("minus_half", "ln_eps", "rms_eps", "one_over_d"))

        x_row = sb("x_row", P, NT, D)
        x_plus = sb("x_plus", P, NT, D)
        squares = sb("squares", P, NT, D)
        sum_sq = sb("sum_sq", P, NT)
        mean_sq = sb("mean_sq", P, NT)
        rms_inv = sb("rms_inv", P, NT)
        h_row = sb("h_row", P, NT, D)
        hT = sb("hT", P, S)
        v_aug = sb("v_aug", P, NT, H, DH + 1)
        qk = sb("qk", P, 2, 2, S)
        neg_max = sb("neg_max", P, H, NT)
        probs = sb("probs", P, 2, NT, S)
        probsT = sb("probsT", P, 2, NT, S)
        row_inv = sb("row_inv", P, NT * 2)
        o_row = sb("o_row", P, 2, NT, 2, DH)
        oT = sb("oT", P, HP, S)
        y1 = sb("y1", P, NT, D)
        x1 = sb("x1", P, NT, D)
        x1T = sb("x1T", P, S)
        hid0 = sb("hid0", P, E + 1, M0, S)
        y2 = sb("y2", P, NT, D)
        x2 = sb("x2", P, NT, D)
        x2_plus = sb("x2_plus", P, NT, D)
        x2T = sb("x2T", P, S)
        qkv1 = sb("qkv1", P, NT, NH1, 3, DH1)
        prod = sb("prod", P, NH1, NH1, DH1)
        score1 = sb("score1", P, NT, NH1, NH1)
        max1 = sb("max1", P, NH1)
        exp1 = sb("exp1", P, NT, NH1, NH1)
        pv1 = sb("pv1", P, NT, NH1, DH1, NH1)
        sum1 = sb("sum1", P, NH1)
        inv1 = sb("inv1", P, NH1)
        ao = sb("ao", P, NT, NH1, DH1)
        aoT = sb("aoT", P, S)
        y3 = sb("y3", P, NT, D)
        x3 = sb("x3", P, NT, D)
        x3T = sb("x3T", P, S)
        hid1 = sb("hid1", P, E, M1, S)
        y4 = sb("y4", P, NT, D)
        x4 = sb("x4", P, NT, D)
        logits = [sb(f"logits{i}", P, NT, E) for i in range(2)]
        top8 = [sb(f"top8_{i}", P, NT, 8) for i in range(2)]
        top2 = [sb(f"top2_{i}", P, NT, 8) for i in range(2)]
        marked = [sb(f"marked{i}", P, NT, E) for i in range(2)]
        shifted = [sb(f"shifted{i}", P, NT, E) for i in range(2)]
        rexp = [sb(f"rexp{i}", P, NT, E) for i in range(2)]
        rsum = [sb(f"rsum{i}", P, NT) for i in range(2)]
        gates = [sb(f"gates{i}", P, NT, E + 1) for i in range(2)]
        gates0T = sb("gates0T", E + 1, S)
        stats = [sb(f"stats{i}", P, NT, 6) for i in range(4)]
        mv = [sb(f"mv{i}", P, NT, 2) for i in range(4)]
        var_eps = [sb(f"var_eps{i}", P, NT) for i in range(4)]
        std_inv = [sb(f"std_inv{i}", P, NT) for i in range(4)]

        banks = {}
        for n in BANKS:
            t = ctx.enter_context(nc.psum_tensor(f"bank_{n}", [P, 512], F32))
            banks[n] = (t, sem(f"filled_{n}"), sem(f"drained_{n}"))

        w_loaded = sem("w_loaded")
        consts_ready = sem("consts_ready")
        wq_scaled = sem("wq_scaled")
        x_loaded = sem("x_loaded")
        sq_ready = sem("sq_ready")
        rms_ready = sem("rms_ready")
        h_ready = sem("h_ready")
        xplus_ready = sem("xplus_ready")
        max_ready = sem("max_ready")
        stats_ready = [sem(f"stats_ready{i}") for i in range(4)]
        std_ready = [sem(f"std_ready{i}") for i in range(4)]
        ln_ready = [sem(f"ln_ready{i}") for i in range(4)]
        shifted_ready = [sem(f"shifted_ready{i}") for i in range(2)]
        rexp_ready = [sem(f"rexp_ready{i}") for i in range(2)]
        gates_ready = sem("gates_ready")
        x2plus_ready = sem("x2plus_ready")
        score_ready = sem("score_ready")
        exp1_ready = sem("exp1_ready")
        pv1_ready = sem("pv1_ready")
        ao_ready = sem("ao_ready")
        stored = sem("stored")

        def run(eng, body, before=None):
            if before:
                before(Before(banks))
            for it in range(FIRST):
                body(Iteration(it, 0, banks))
            with eng.Fori(0, LAST - FIRST + 1) as step:
                body(Iteration(FIRST, step, banks))
            for it in range(LAST + 1, ROWS + 2):
                body(Iteration(it, 0, banks))

        def settled(eng, step):
            eng.drain()

        n_loads = [0]
        block = ctx.enter_context(nc.Block())

        @block.sync
        def _(sp):
            def load(dst, src):
                sp.dma_start(dst, src).then_inc(w_loaded, 16)
                n_loads[0] += 16

            def load_x(row):
                sp.dma_start(x_row[:], x_in[row, :, :].rearrange("(t p) d -> p t d", p=P)).then_inc(x_loaded, 16)

            def replicate(src, n):
                return bass.AP(src.tensor, src.offset, [[0, P], [1, n]])

            load_x(0)
            sp.dma_start(nscale[:], norm_scale.rearrange("(p a) -> p a", a=1)).then_inc(stored, 16)
            for dst, src in ((wv, wv_in), (wq, wq_in), (wk, wk_in)):
                load(dst[:], src.rearrange("d h e -> d (h e)"))
            load(wo[:], wo_in.rearrange("h e d -> (h e) d").rearrange("(s p) d -> p s d", p=P))
            load(b_out[:, 0, :], replicate(b_out_in, D))
            load(bproj[:, 0, :], replicate(bproj_in, D))
            load(router0_b[:, 0, :], replicate(router0_b_in, E))
            load(router0[:], router0_in)
            load(router1[:], router1_in)
            load(up0[:, 0:E, :], rw1_in.rearrange("e d h -> d e h"))
            load(up0[:, E, :], sw1_in)
            load(up0_b[:, 0:E, :], rb1_in)
            load(up0_b[:, E, :], sb1_in)
            load(down0[:, 0:E, :, :].rearrange("p e k d -> p (e k) d"), rw2_in.rearrange("e h d -> (e h) d").rearrange("(k p) d -> p k d", p=P))
            load(down0[:, E, :, :], sw2_in.rearrange("(k p) d -> p k d", p=P))
            load(down0_b[0:E, :], rb2_in)
            load(down0_b[E:E + 1, :], sb2_in.rearrange("(a d) -> a d", a=1))
            load(wqkv1[:], wqkv1_in)
            load(wproj[:], wproj_in)
            load(up1[:], w1_in)
            load(down1[:], w2_in)

            def body(v):
                if v.next:
                    sp.wait_ge(h_ready, v.at(0, 1, 1))
                    sp.wait_ge(xplus_ready, v.at(0, 1, 1))
                    load_x(v.it + 1 + v.step)
                if v.c:
                    sp.wait_ge(ln_ready[3], v.at(2, 1, 1))
                    sp.dma_start(out[v.it - 2 + v.step, :, :].rearrange("(t p) d -> p t d", p=P), x4[:]).then_inc(stored, 16)

            run(sp, body)
            sp.wait_ge(stored, 16 * (ROWS + 1))

        @block.gpsimd
        def _(pool):
            g = nc.gpsimd
            g.memset(ident[:], 0.0).then_inc(consts_ready, 1)
            pool.wait_ge(consts_ready, 1)
            g.affine_select(out=ident[:], in_=ident[:], compare_op=ALU.not_equal, fill=1.0, base=0,
                            pattern=[[-1, P]], channel_multiplier=1)
            g.memset(minus_half[:], -0.5)
            g.memset(v_aug[:, :, :, DH:DH + 1], 1.0)
            for i in range(2):
                g.memset(top2[i][:], -3.0e38)
                g.memset(gates[i][:, :, E:E + 1], 1.0)
            g.memset(ln_eps[:], LN_EPS)
            g.memset(rms_eps[:], RMS_EPS)
            g.memset(one_over_d[:], 1.0 / D).then_inc(consts_ready, 1)
            pool.wait_ge(consts_ready, 2)
            pool.wait_ge(w_loaded, n_loads[0])

            def inverse_std(v, i, lag):
                pool.wait_ge(stats_ready[i], v.at(lag, 1, 1))
                settled(pool, g.tensor_tensor(var_eps[i][:], mv[i][:, :, 1], ln_eps[:], ALU.add))
                g.tensor_tensor(std_inv[i][:], var_eps[i][:], minus_half[:], ALU.pow).then_inc(std_ready[i], 1)

            def rms(v):
                pool.wait_ge(sq_ready, v.at(-1, 1, 1))
                settled(pool, g.tensor_tensor(mean_sq[:], sum_sq[:], one_over_d[:], ALU.mult))
                settled(pool, g.tensor_tensor(mean_sq[:], mean_sq[:], rms_eps[:], ALU.add))
                g.tensor_tensor(rms_inv[:], mean_sq[:], minus_half[:], ALU.pow).then_inc(rms_ready, 1)

            def plus(v):
                pool.wait_ge(x_loaded, v.at(-1, 16, 16))
                if v.a:
                    pool.wait_ge(*v.drain("OUT"))
                g.tensor_tensor(x_plus[:], x_row[:], b_out[:, 0:1, :].broadcast_to([P, NT, D]), ALU.add).then_inc(xplus_ready, 1)

            def body(v):
                if v.b:
                    inverse_std(v, 1, 1)
                    pool.wait_ge(ln_ready[1], v.at(1, 1, 1))
                    g.tensor_tensor(x2_plus[:], x2[:], bproj[:, 0:1, :].broadcast_to([P, NT, D]), ALU.add).then_inc(x2plus_ready, 1)
                    for t in range(NT):
                        pool.wait_ge(exp1_ready, v.at(1, NT, t + 1))
                        for half in range(2):
                            hs = slice(half * 8, half * 8 + 8)
                            ins = g.tensor_tensor(
                                pv1[:, t, hs], exp1[:, t, hs].rearrange("p h (a g) -> p h a g", a=1).broadcast_to([P, 8, DH1, NH1]),
                                qkv1[:, t, :, 2, :].rearrange("p g (a d) -> p a d g", a=1).broadcast_to([P, 8, DH1, NH1]), ALU.mult)
                        ins.then_inc(pv1_ready, 1)
                if v.c:
                    inverse_std(v, 3, 2)
                if v.b:
                    inverse_std(v, 2, 1)
                if v.a:
                    inverse_std(v, 0, 0)
                if v.next:
                    rms(v)
                    plus(v)

            def before(v):
                rms(v)
                plus(v)

            run(pool, body, before)

        @block.scalar
        def _(act):
            sc = nc.scalar
            act.wait_ge(w_loaded, n_loads[0])
            act.wait_ge(consts_ready, 2)
            sc.activation(wq[:], wq[:], ACT.Copy, scale=float(DH) ** -0.5).then_inc(wq_scaled, 1)

            def squares_of(v):
                act.wait_ge(x_loaded, v.at(-1, 16, 16))
                for t in range(NT):
                    ins = sc.activation(squares[:, t, :], x_row[:, t, :], ACT.Square, accum_out=sum_sq[:, t:t + 1])
                ins.then_inc(sq_ready, 1)

            def copy_out(v, name, dst, src):
                act.wait_ge(*v.fill(name))
                sc.activation(dst, src, ACT.Copy).then_inc(v.drain(name)[0], 1)

            def v_out(v, n):
                t, half = n // 2, n % 2
                copy_out(v, f"V{n}", v_aug[:, t, half * 8:half * 8 + 8, 0:DH],
                         v.bank(f"V{n}")[:, :].rearrange("p (h e) -> p h e", e=DH))

            def qk_out(v, s):
                copy_out(v, f"QK{s}", qk[:, s % 2], v.bank(f"QK{s}")[:, :].rearrange("p (a n) -> p a n", a=2))

            def softmax_exp(v, h):
                act.wait_ge(max_ready, v.at(0, H, h + 1))
                for t in range(NT):
                    ins = sc.activation(probs[:, h % 2, t, :], v.bank(f"S{h}")[:, t * S:(t + 1) * S], ACT.Exp,
                                        bias=neg_max[:, h, t:t + 1])
                ins.then_inc(v.drain(f"S{h}")[0], 1)

            def probsT_out(v, h):
                copy_out(v, f"T{h}", probsT[:, h % 2], v.bank(f"T{h}")[:, :].rearrange("p (k q) -> p k q", k=NT))

            def router_exp(v, i):
                lag = i + 1
                act.wait_ge(shifted_ready[i], v.at(lag, 1, 1))
                sc.activation(rexp[i][:], shifted[i][:], ACT.Exp).then_inc(rexp_ready[i], 1)

            def head_exp(v, t):
                act.wait_ge(score_ready, v.at(1, NT, t + 1))
                sc.activation(exp1[:, t], score1[:, t], ACT.Exp, scale=1.0 / 8.0).then_inc(exp1_ready, 1)

            def gelu0(v, u):
                act.wait_ge(*v.fill(f"U0_{u}"))
                for m in range(M0):
                    ins = sc.activation(hid0[:, u, m, :], v.bank(f"U0_{u}")[:, m * S:(m + 1) * S], ACT.Gelu,
                                        bias=up0_b[:, u, m:m + 1])
                ins.then_inc(v.drain(f"U0_{u}")[0], 1)

            def gelu1(v, u):
                act.wait_ge(*v.fill(f"U1_{u}"))
                e, m = u // 2, u % 2 * 2
                sc.activation(hid1[:, e, m:m + 2, :], v.bank(f"U1_{u}")[:, :].rearrange("p (m n) -> p m n", m=2),
                              ACT.Gelu).then_inc(v.drain(f"U1_{u}")[0], 1)

            def body(v):
                if v.b:
                    router_exp(v, 0)
                if v.c:
                    router_exp(v, 1)
                if v.a:
                    for n in range(4):
                        v_out(v, n)
                    qk_out(v, 0)
                    qk_out(v, 1)
                    softmax_exp(v, 0)
                    softmax_exp(v, 1)
                for s in range(HP):
                    if v.a:
                        probsT_out(v, 2 * s + 1)
                        if s + 2 < HP:
                            qk_out(v, s + 2)
                        if s + 1 < HP:
                            softmax_exp(v, 2 * s + 2)
                            softmax_exp(v, 2 * s + 3)
                    if v.b:
                        if s == 2:
                            copy_out(v, "X2T", x2T[:], v.bank("X2T")[:, 0:S])
                        if s == 3:
                            for t in range(NT):
                                copy_out(v, f"LQ{t}", qkv1[:, t].rearrange("p h c d -> p (h c d)"), v.bank(f"LQ{t}")[:, 0:3 * D])
                        if s == 4:
                            head_exp(v, 0)
                        if s == 5:
                            head_exp(v, 1)
                        if s == 7:
                            copy_out(v, "AOT", aoT[:], v.bank("AOT")[:, 0:S])
                    if v.a and s:
                        copy_out(v, f"OT{s - 1}", oT[:, s - 1, :], v.bank(f"OT{s - 1}")[:, 0:S])
                if v.a:
                    copy_out(v, f"OT{HP - 1}", oT[:, HP - 1, :], v.bank(f"OT{HP - 1}")[:, 0:S])
                if v.b:
                    copy_out(v, "X3T", x3T[:], v.bank("X3T")[:, 0:S])
                    for u in range(2 * E):
                        gelu1(v, u)
                if v.next:
                    squares_of(v)
                if v.a:
                    for u in range(E + 1):
                        gelu0(v, u)

            run(act, body, squares_of)

        @block.vector
        def _(dve):
            ve = nc.vector
            dve.wait_ge(w_loaded, n_loads[0])
            dve.wait_ge(stored, 16)
            dve.wait_ge(consts_ready, 2)

            def head_max(v, h):
                dve.wait_ge(*v.fill(f"S{h}"))
                ve.tensor_reduce(neg_max[:, h, :], v.bank(f"S{h}")[:, :].rearrange("p (t k) -> p t k", t=NT),
                                 AX.X, ALU.max, negate=True).then_inc(max_ready, 1)

            def probsT_out(v, h):
                dve.wait_ge(*v.fill(f"T{h}"))
                ve.tensor_copy(probsT[:, h % 2], v.bank(f"T{h}")[:, :].rearrange("p (k q) -> p k q", k=NT)).then_inc(v.drain(f"T{h}")[0], 1)

            def o_out(v, s):
                dve.wait_ge(*v.fill(f"O{s}"))
                o = v.bank(f"O{s}")[:, 0:NT * 2 * (DH + 1)].rearrange("p (n e) -> p n e", e=DH + 1)
                settled(dve, ve.reciprocal(row_inv[:], o[:, :, DH]))
                ve.tensor_tensor(o_row[:, s % 2].rearrange("p t j e -> p (t j) e"), o[:, :, 0:DH],
                                 row_inv[:].rearrange("p (n a) -> p n a", a=1).broadcast_to([P, NT * 2, DH]),
                                 ALU.mult).then_inc(v.drain(f"O{s}")[0], 1)

            def ln_stats(v, i, y, lag):
                for t in range(NT):
                    settled(dve, ve.bn_stats(stats[i][:, t, :], y[:, t, :]))
                for t in range(NT):
                    ins = ve.bn_aggr(mv[i][:, t, :], stats[i][:, t, :])
                ins.then_inc(stats_ready[i], 1)

            def ln_apply(v, i, y, dst, lag):
                dve.wait_ge(std_ready[i], v.at(lag, 1, 1))
                for t in range(NT):
                    ins = ve.tensor_scalar(dst[:, t, :], y[:, t, :], mv[i][:, t, 0:1], std_inv[i][:, t:t + 1],
                                           ALU.subtract, ALU.mult)
                ins.then_inc(ln_ready[i], 1)

            def route(v, i):
                for t in range(NT):
                    settled(dve, ve.max(top8[i][:, t, :], logits[i][:, t, :]))
                settled(dve, ve.tensor_copy(top2[i][:, :, 0:2], top8[i][:, :, 0:2]))
                for t in range(NT):
                    settled(dve, ve.match_replace(marked[i][:, t, :], top2[i][:, t, :], logits[i][:, t, :], -3.0e38))
                ve.tensor_tensor(shifted[i][:], logits[i][:], top8[i][:, :, 0:1].broadcast_to([P, NT, E]),
                                 ALU.subtract).then_inc(shifted_ready[i], 1)
                settled(dve, ve.tensor_tensor(marked[i][:], marked[i][:], logits[i][:], ALU.not_equal))

            def gate(v, i, lag):
                dve.wait_ge(rexp_ready[i], v.at(lag, 1, 1))
                settled(dve, ve.reduce_sum(rsum[i][:], rexp[i][:], AX.X))
                settled(dve, ve.reciprocal(rsum[i][:], rsum[i][:]))
                settled(dve, ve.tensor_tensor(marked[i][:], marked[i][:], rexp[i][:], ALU.mult))
                ins = ve.tensor_tensor(gates[i][:, :, 0:E], marked[i][:], rsum[i][:].rearrange("p (t a) -> p t a", a=1).broadcast_to([P, NT, E]),
                                       ALU.mult)
                if i == 0:
                    ins.then_inc(gates_ready, 1)
                settled(dve, ins)

            def mix(v, name, i, pair, acc, first):
                dve.wait_ge(*v.fill(name))
                y = v.bank(name)[:, :].rearrange("p (j t d) -> p j t d", j=2, t=NT)
                for j in range(2):
                    for t in range(NT):
                        e = 2 * pair + j
                        src = first if first is not None and j == 0 else acc
                        ins = ve.scalar_tensor_tensor(acc[:, t, :], y[:, j, t, :], gates[i][:, t, e:e + 1], src[:, t, :],
                                                      ALU.mult, ALU.add)
                        if j == 1 and t == NT - 1:
                            ins.then_inc(v.drain(name)[0], 1)
                        settled(dve, ins)

            def head_scores(v, t):
                dve.wait_ge(*v.drain(f"LQ{t}"))
                full = [P, NH1, NH1, DH1]
                q = qkv1[:, t, :, 0, :].rearrange("p h (a d) -> p h a d", a=1).broadcast_to(full)
                k = qkv1[:, t, :, 1, :].rearrange("p (a g) d -> p a g d", a=1).broadcast_to(full)
                settled(dve, ve.tensor_tensor(prod[:], q, k, ALU.mult))
                settled(dve, ve.reduce_sum(score1[:, t], prod[:], AX.X))
                settled(dve, ve.reduce_max(max1[:], score1[:, t], AX.X))
                ve.tensor_tensor(score1[:, t], score1[:, t], max1[:].rearrange("p (h a) -> p h a", a=1).broadcast_to([P, NH1, NH1]),
                                 ALU.subtract).then_inc(score_ready, 1)

            def head_mix(v, t):
                dve.wait_ge(exp1_ready, v.at(1, NT, t + 1))
                settled(dve, ve.reduce_sum(sum1[:], exp1[:, t], AX.X))
                settled(dve, ve.reciprocal(inv1[:], sum1[:]))
                dve.wait_ge(pv1_ready, v.at(1, NT, t + 1))
                settled(dve, ve.reduce_sum(ao[:, t], pv1[:, t], AX.X))
                ve.tensor_tensor(ao[:, t], ao[:, t], inv1[:].rearrange("p (h a) -> p h a", a=1).broadcast_to([P, NH1, DH1]),
                                 ALU.mult).then_inc(ao_ready, 1)

            def input_norm(v):
                dve.wait_ge(rms_ready, v.at(-1, 1, 1))
                dve.wait_ge(x_loaded, v.at(-1, 16, 16))
                for t in range(NT):
                    ins = ve.tensor_scalar(h_row[:, t, :], x_row[:, t, :], rms_inv[:, t:t + 1], None, ALU.mult)
                ins.then_inc(h_ready, 1)
                dve.wait_ge(*v.fill("HT"))
                ve.tensor_scalar(hT[:], v.bank("HT")[:, 0:S], nscale[:, 0:1], None, ALU.mult).then_inc(v.drain("HT")[0], 1)

            def body(v):
                if v.b:
                    gate(v, 0, 1)
                    dve.wait_ge(*v.fill("WT0"))
                    ve.tensor_copy(gates0T[:], v.bank("WT0")[0:E + 1, 0:S]).then_inc(v.drain("WT0")[0], 1)
                if v.c:
                    gate(v, 1, 2)
                if v.a:
                    head_max(v, 0)
                    head_max(v, 1)
                for s in range(HP):
                    if v.a:
                        probsT_out(v, 2 * s)
                        if s + 1 < HP:
                            head_max(v, 2 * s + 2)
                            head_max(v, 2 * s + 3)
                    if v.b:
                        if s == 0:
                            dve.wait_ge(*v.fill("D0base"))
                            ve.tensor_tensor(y2[:], v.bank("D0base")[:, 0:NT * D].rearrange("p (t d) -> p t d", t=NT),
                                             x1[:], ALU.add).then_inc(v.drain("D0base")[0], 1)
                            dve.drain()
                            mix(v, "D0p0", 0, 0, y2, None)
                            mix(v, "D0p1", 0, 1, y2, None)
                        if s == 1:
                            mix(v, "D0p2", 0, 2, y2, None)
                            mix(v, "D0p3", 0, 3, y2, None)
                            ln_stats(v, 1, y2, 1)
                            ln_apply(v, 1, y2, x2, 1)
                        if s == 3:
                            head_scores(v, 0)
                        if s == 4:
                            head_scores(v, 1)
                        if s == 5:
                            head_mix(v, 0)
                        if s == 6:
                            head_mix(v, 1)
                    if v.c:
                        if s >= 3 and s < 7:
                            mix(v, f"D1p{s - 3}", 1, s - 3, y4, x3 if s == 3 else None)
                        if s == 7:
                            ln_stats(v, 3, y4, 2)
                    if v.b and s == 7:
                        dve.wait_ge(*v.fill("PROJ"))
                        dve.wait_ge(x2plus_ready, v.at(1, 1, 1))
                        ve.tensor_tensor(y3[:], v.bank("PROJ")[:, 0:NT * D].rearrange("p (t d) -> p t d", t=NT),
                                         x2_plus[:], ALU.add).then_inc(v.drain("PROJ")[0], 1)
                        dve.drain()
                        ln_stats(v, 2, y3, 1)
                    if v.a:
                        o_out(v, s)
                if v.b:
                    ln_apply(v, 2, y3, x3, 1)
                if v.c:
                    dve.wait_ge(stored, v.at(2, 16, 16))
                    ln_apply(v, 3, y4, x4, 2)
                if v.a:
                    dve.wait_ge(*v.fill("OUT"))
                    dve.wait_ge(xplus_ready, v.at(0, 1, 1))
                    ve.tensor_tensor(y1[:], v.bank("OUT")[:, 0:NT * D].rearrange("p (t d) -> p t d", t=NT),
                                     x_plus[:], ALU.add).then_inc(v.drain("OUT")[0], 1)
                    dve.drain()
                    ln_stats(v, 0, y1, 0)
                    ln_apply(v, 0, y1, x1, 0)
                if v.b:
                    dve.wait_ge(*v.fill("R1"))
                    ve.tensor_copy(logits[1][:], v.bank("R1")[:, 0:NT * E].rearrange("p (t e) -> p t e", t=NT)).then_inc(v.drain("R1")[0], 1)
                if v.a:
                    dve.wait_ge(*v.fill("X1T"))
                    ve.tensor_copy(x1T[:], v.bank("X1T")[:, 0:S]).then_inc(v.drain("X1T")[0], 1)
                    dve.wait_ge(*v.fill("R0"))
                    ve.tensor_tensor(logits[0][:], v.bank("R0")[:, 0:NT * E].rearrange("p (t e) -> p t e", t=NT),
                                     router0_b[:, 0:1, :].broadcast_to([P, NT, E]), ALU.add).then_inc(v.drain("R0")[0], 1)
                    dve.drain()
                    route(v, 0)
                if v.b:
                    dve.drain()
                    route(v, 1)
                if v.next:
                    input_norm(v)

            run(dve, body, input_norm)

        @block.tensor
        def _(pe):
            te = nc.tensor
            pe.wait_ge(consts_ready, 2)
            pe.wait_ge(w_loaded, n_loads[0])
            pe.wait_ge(wq_scaled, 1)

            def tokens(t):
                return slice(t * P, (t + 1) * P)

            def transpose_row(bank, src):
                for t in range(NT):
                    ins = te.transpose(bank[0:src.shape[2], tokens(t)], src[:, t, :], ident[:])
                return ins

            def wait_drained(v, name, source):
                if v.nth[source][0] != v.nth[name][0]:
                    pe.wait_ge(*v.drain(source))

            def unit(v, name):
                bank = v.bank(name)

                if name[0] == "V":
                    n = int(name[1:])
                    pe.wait_ge(*drained_ht(v))
                    return te.matmul(bank[:, :], hT[:, tokens(n // 2)], wv[:, n % 2 * 512:n % 2 * 512 + 512], start=True, stop=True)
                if name[:2] == "QK":
                    s = int(name[2:])
                    te.matmul(bank[:, 0:S], wq[:, tokens(s)], hT[:], start=True, stop=True)
                    return te.matmul(bank[:, S:2 * S], wk[:, tokens(s)], hT[:], start=True, stop=True)
                if name[0] == "S":
                    h = int(name[1:])
                    s, r = h // 2, slice(h % 2 * DH, h % 2 * DH + DH)
                    wait_drained(v, name, f"QK{s}")
                    for t in range(NT):
                        ins = te.matmul(bank[:, t * S:(t + 1) * S], qk[r, s % 2, 0, tokens(t)], qk[r, s % 2, 1, :], start=True, stop=True)
                    return ins
                if name[0] == "T":
                    h = int(name[1:])
                    pe.wait_ge(*v.drain(f"S{h}"))
                    for k in range(NT):
                        for t in range(NT):
                            ins = te.transpose(bank[:, k * S + t * P:k * S + (t + 1) * P], probs[:, h % 2, t, tokens(k)], ident[:])
                    return ins
                if name[:2] == "OT":
                    s = int(name[2:])
                    wait_drained(v, name, f"O{s}")
                    return transpose_row(bank, o_row[:, s % 2].rearrange("p t j e -> p t (j e)"))
                if name == "OUT":
                    wait_drained(v, name, f"OT{HP - 1}")
                    for t in range(NT):
                        for s in range(HP):
                            ins = te.matmul(bank[:, tokens(t)], oT[:, s, tokens(t)], wo[:, s, :], start=s == 0, stop=s == HP - 1)
                    return ins
                if name[0] == "O":
                    s = int(name[1:])
                    for j in range(2):
                        h = 2 * s + j
                        wait_drained(v, name, f"T{h}")
                        for t in range(NT):
                            col = (t * 2 + j) * (DH + 1)
                            for k in range(NT):
                                ins = te.matmul(bank[:, col:col + DH + 1], probsT[:, j, k, tokens(t)], v_aug[:, k, h, :],
                                                start=k == 0, stop=k == NT - 1)
                    return ins
                if name == "X1T":
                    pe.wait_ge(ln_ready[0], v.at(0, 1, 1))
                    return transpose_row(bank, x1)
                if name == "X2T":
                    pe.wait_ge(ln_ready[1], v.at(1, 1, 1))
                    return transpose_row(bank, x2)
                if name == "X3T":
                    pe.wait_ge(ln_ready[2], v.at(1, 1, 1))
                    return transpose_row(bank, x3)
                if name == "HT":
                    pe.wait_ge(h_ready, v.at(-1, 1, 1))
                    return transpose_row(bank, h_row)
                if name in ("R0", "R1"):
                    xT, w = ((x1T, router0), (x3T, router1))[int(name[1])]
                    wait_drained(v, name, "X1T" if name == "R0" else "X3T")
                    for t in range(NT):
                        ins = te.matmul(bank[:, t * E:(t + 1) * E], xT[:, tokens(t)], w[:], start=True, stop=True)
                    return ins
                if name == "WT0":
                    pe.wait_ge(gates_ready, v.at(1, 1, 1))
                    return transpose_row(bank, gates[0])
                if name[:3] == "U0_":
                    e = int(name[3:])
                    for m in range(M0):
                        ins = te.matmul(bank[:, m * S:(m + 1) * S], up0[:, e, tokens(m)], x1T[:], start=True, stop=True)
                    return ins
                if name[:3] == "U1_":
                    u = int(name[3:])
                    for m in range(2):
                        ins = te.matmul(bank[:, m * S:(m + 1) * S], up1[:, u // 2, tokens(u % 2 * 2 + m)], x3T[:], start=True, stop=True)
                    return ins
                if name == "D0base":
                    wait_drained(v, name, "WT0")
                    for t in range(NT):
                        for k in range(M0):
                            te.matmul(bank[:, tokens(t)], hid0[:, E, k, tokens(t)], down0[:, E, k, :], start=k == 0, stop=False)
                        ins = te.matmul(bank[:, tokens(t)], gates0T[:, tokens(t)], down0_b[:], start=False, stop=True)
                    return ins
                if name[:3] in ("D0p", "D1p"):
                    hid, down, m = ((hid0, down0, M0), (hid1, down1, M1))[int(name[1])]
                    for j in range(2):
                        e = 2 * int(name[3:]) + j
                        for t in range(NT):
                            for k in range(m):
                                ins = te.matmul(bank[:, (j * NT + t) * P:(j * NT + t + 1) * P], hid[:, e, k, tokens(t)],
                                                down[:, e, k, :], start=k == 0, stop=k == m - 1)
                    return ins
                if name in ("LQ0", "LQ1"):
                    t = int(name[2])
                    wait_drained(v, name, "X2T")
                    return te.matmul(bank[:, 0:3 * D], x2T[:, tokens(t)], wqkv1[:], start=True, stop=True)
                if name == "AOT":
                    pe.wait_ge(ao_ready, v.at(1, NT, NT))
                    return transpose_row(bank, ao[:].rearrange("p t h d -> p t (h d)"))
                assert name == "PROJ"
                wait_drained(v, name, "AOT")
                for t in range(NT):
                    ins = te.matmul(bank[:, tokens(t)], aoT[:, tokens(t)], wproj[:], start=True, stop=True)
                return ins

            def drained_ht(v):
                if v.it == 0:
                    return banks["A0"][2], 1
                bank, n = Iteration(v.it - 1, v.step, banks).nth["HT"]
                return banks[bank][2], n + v.step * v.per[bank]

            def body(v):
                for name, bank in (pe_units(v.it) if v.it >= 0 else PRE):
                    free, count = v.drain(name, before=1)
                    if v.it > 0 or count:
                        pe.wait_ge(free, count)
                    unit(v, name).then_inc(v.fill(name)[0], 1)

            run(pe, body, body)


def kernel(**inputs):
    import numpy as np
    import concourse.bacc as bacc
    from concourse import mybir as mb
    from concourse.bass_utils import run_bass_kernel_spmd

    i = {k: np.asarray(v) for k, v in inputs.items()}
    E_, H0, H1 = 8, 256, 512
    arrays = {
        "x": i["L0_attn_x"], "norm_scale": i["L0_attn_norm_scale"], "wq": i["L0_attn_wq"], "wk": i["L0_attn_wk"],
        "wv": i["L0_attn_wv"], "wo": i["L0_attn_w_out"], "b_out": i["L0_attn_b_out"],
        "router0": i["L0_ffn_router_w"], "router0_b": i["L0_ffn_router_b"], "sw1": i["L0_ffn_sw1"],
        "sb1": i["L0_ffn_sb1"].reshape(H0 // 128, 128).transpose(1, 0), "sw2": i["L0_ffn_sw2"], "sb2": i["L0_ffn_sb2"],
        "rw1": i["L0_ffn_rw1"], "rb1": i["L0_ffn_rb1"].reshape(E_, H0 // 128, 128).transpose(2, 0, 1),
        "rw2": i["L0_ffn_rw2"], "rb2": i["L0_ffn_rb2"],
        "wqkv1": i["L1_attn_Wqkv"].transpose(1, 0), "wproj": i["L1_attn_Wproj"].transpose(1, 0), "bproj": i["L1_attn_bproj"],
        "router1": i["L1_ffn_router_w"].transpose(1, 0), "w1": i["L1_ffn_w1"].transpose(2, 0, 1),
        "w2": i["L1_ffn_w2"].reshape(E_, 128, H1 // 128, 128).transpose(3, 0, 2, 1),
    }
    arrays = {f"in_{k}": np.ascontiguousarray(v) for k, v in arrays.items()}
    nc = bacc.Bacc("TRN2", target_bir_lowering=False, num_devices=1)
    args = [nc.dram_tensor(k, v.shape, mb.dt.from_np(v.dtype), kind="ExternalInput").ap() for k, v in arrays.items()]
    out = nc.dram_tensor("out", (16, 256, 128), mb.dt.from_np(np.dtype("float32")), kind="ExternalOutput").ap()
    transformer_blocks(nc, *args, out)
    r = run_bass_kernel_spmd(nc, [arrays], core_ids=[0])
    return r.results[0]["out"]
```

```python
import concourse.bass as bass
from concourse import mybir
from contextlib import ExitStack

F32 = mybir.dt.float32
ALU = mybir.AluOpType
ACT = mybir.ActivationFunctionType
AX = mybir.AxisListType

P = 128
ROWS, S, D = 16, 256, 128
NT = S // P
H, DH = 16, 64
HP = H // 2
E = 8
HID0, HID1 = 256, 512
M0, M1 = HID0 // P, HID1 // P
NH1, DH1 = 16, 8
LN_EPS, RMS_EPS = 1e-5, 1e-6
FIRST, LAST = 2, ROWS - 2



FILL_B = {(0, 0): ["WT0"], (0, 1): ["D0p0"], (1, 0): ["D0p1"], (1, 1): ["D0p2"],
          (2, 0): ["D0p3", "D0base"], (3, 0): ["X2T"], (3, 1): ["LQ0", "LQ1"]}
FILL_C = {(2, 1): ["D1e0"], (3, 0): ["D1e1"], (4, 0): ["D1e2"], (5, 0): ["D1e3"], (6, 0): ["D1e4"],
          (7, 1): ["D1e5"]}


def fill_units(it, s, place):
    b, c = 1 <= it <= ROWS, 2 <= it <= ROWS + 1
    return (FILL_B.get((s, place), []) if b else []) + (FILL_C.get((s, place), []) if c else [])


def pe_units(it):
    a, b, c, nxt = it < ROWS, 1 <= it <= ROWS, 2 <= it <= ROWS + 1, it < ROWS - 1
    order = []
    rings = {"A": ["A0", "A1"], "F": ["F0", "F1"], "G": ["F0", "F1", "T0", "T1"]}
    turn = {k: 0 for k in rings}

    def put(ring, *names, on=True):
        for name in names if on else ():
            banks = rings.get(ring, [ring])
            order.append((name, banks[turn.get(ring, 0) % len(banks)]))
            if ring in turn:
                turn[ring] += 1

    put("A", "QK0", "V0", on=a)
    put("S0", "S0", on=a)
    put("S1", "S1", on=a)
    put("A", "QK1", "V1", "V2", "V3", on=a)
    for s in range(HP):
        put("S0", f"S{2 * s + 2}", on=a and s + 1 < HP)
        put("S1", f"S{2 * s + 3}", on=a and s + 1 < HP)
        put("A", f"O{s - 1}", on=a and s >= 1)
        put("F", *fill_units(it, s, 0))
        put("T0", f"T{2 * s}", on=a)
        put("T1", f"T{2 * s + 1}", on=a)
        put("A", f"QK{s + 2}", on=a and s + 2 < HP)
        put("F", *fill_units(it, s, 1))
    put("A", f"O{HP - 1}", "OUT", on=a)
    put("F", "D1e6", "D1e7", on=c)
    put("A", "X1T", on=a)
    put("G", "U0_0", "U0_1", on=a)
    put("A", "R0", on=a)
    put("G", "U0_2", "U0_3", on=a)
    put("G", "AOT", on=b)
    put("G", "U0_4", on=a)
    put("G", "PROJ", on=b)
    put("G", "U0_5", "U0_6", "U0_7", on=a)
    put("G", "X3T", on=b)
    put("G", "U0_8", on=a)
    put("G", "U1_0", "U1_1", "U1_2", "R1", on=b)
    put("G", *[f"U1_{u}" for u in range(3, 2 * E - 4)], on=b)
    put("A", "HT", on=nxt)
    put("G", *[f"U1_{u}" for u in range(2 * E - 4, 2 * E)], on=b)
    return order


PRE = [("HT", "A0")]
BANKS = ["S0", "S1", "T0", "T1", "A0", "A1", "F0", "F1"]


def count_units(it):
    seen = {k: 0 for k in BANKS}
    for units in [PRE] + [pe_units(i) for i in range(it)]:
        for _, bank in units:
            seen[bank] += 1
    return seen


class Iteration:

    def __init__(self, it, step, banks):
        self.it, self.step, self.banks = it, step, banks
        self.a, self.b, self.c = it < ROWS, 1 <= it <= ROWS, 2 <= it <= ROWS + 1
        self.next = it < ROWS - 1
        seen, self.nth = count_units(it), {}
        self.per = {k: 0 for k in BANKS}
        for name, bank in pe_units(it):
            seen[bank] += 1
            self.per[bank] += 1
            self.nth[name] = (bank, seen[bank])

    def at(self, lag, per, k):
        return (self.it - lag) * per + k + self.step * per

    def fill(self, name, before=0):
        bank, n = self.nth[name]
        return self.banks[bank][1], n - before + self.step * self.per[bank]

    def drain(self, name, before=0):
        bank, n = self.nth[name]
        return self.banks[bank][2], n - before + self.step * self.per[bank]

    def bank(self, name):
        return self.banks[self.nth[name][0]][0]


class Before(Iteration):

    def __init__(self, banks):
        self.it, self.step, self.banks = -1, 0, banks
        self.a = self.b = self.c = False
        self.next = True
        self.nth, self.per = {"HT": ("A0", 1)}, {k: 0 for k in BANKS}


def transformer_blocks(nc, x_in, norm_scale, wq_in, wk_in, wv_in, wo_in, b_out_in,
                       router0_in, router0_b_in, sw1_in, sb1_in, sw2_in, sb2_in, rw1_in, rb1_in, rw2_in,
                       rb2_in, wqkv1_in, wproj_in, bproj_in, router1_in, w1_in, w2_in, out):
    ctx = ExitStack()
    with ctx:
        def sb(name, *shape):
            return ctx.enter_context(nc.sbuf_tensor(name, list(shape), F32))

        def sem(name):
            return ctx.enter_context(nc.semaphore(name))

        wq, wk, wv = (sb(n, P, H * DH) for n in ("wq", "wk", "wv"))
        wo = sb("wo", P, HP, D)
        nscale = sb("nscale", P, 1)
        b_out = sb("b_out", P, 1, D)
        bproj = sb("bproj", P, 1, D)
        router0 = sb("router0", P, E)
        router0_b = sb("router0_b", P, 1, E)
        router1 = sb("router1", P, E)
        up0 = sb("up0", P, E + 1, HID0)
        up0_b = sb("up0_b", P, E + 1, M0)
        down0 = sb("down0", P, E + 1, M0, D)
        down0_b = sb("down0_b", E + 1, D)
        wqkv1 = sb("wqkv1", P, 3 * D)
        wproj = sb("wproj", P, D)
        up1 = sb("up1", P, E, HID1)
        down1 = sb("down1", P, E, M1, D)
        ident = sb("ident", P, P)
        minus_half, ln_eps, rms_eps, one_over_d = (sb(n, P, NT) for n in ("minus_half", "ln_eps", "rms_eps", "one_over_d"))

        x_row = sb("x_row", P, NT, D)
        x_plus = sb("x_plus", P, NT, D)
        squares = sb("squares", P, NT, D)
        sum_sq = sb("sum_sq", P, NT)
        mean_sq = sb("mean_sq", P, NT)
        rms_inv = sb("rms_inv", P, NT)
        h_row = sb("h_row", P, NT, D)
        hT = sb("hT", P, S)
        values = sb("values", P, NT, H * DH)
        qk = sb("qk", P, 2, 2, S)
        neg_max = sb("neg_max", P, H, NT)
        probs = sb("probs", P, 2, 2, NT, S)
        probsT = sb("probsT", P, 2, NT, S)
        row_sum = sb("row_sum", P, 2, 2 * NT)
        row_inv = sb("row_inv", P, 2, 2 * NT)
        oT = sb("oT", P, HP, S)
        y1 = sb("y1", P, NT, D)
        x1 = sb("x1", P, NT, D)
        x1T = sb("x1T", P, S)
        hid0 = sb("hid0", P, E + 1, M0, S)
        y2 = sb("y2", P, NT, D)
        x2 = sb("x2", P, NT, D)
        x2_plus = sb("x2_plus", P, NT, D)
        x2T = sb("x2T", P, S)
        qkv1 = sb("qkv1", P, NT, NH1, 3, DH1)
        prod = sb("prod", P, NT, NH1, NH1, DH1)
        score1 = sb("score1", P, NT, NH1, NH1)
        max1 = sb("max1", P, NH1)
        exp1 = sb("exp1", P, NT, NH1, NH1)
        pv1 = prod[:].rearrange("p t h (d x) c -> p t h d (x c)", d=DH1)
        sum1 = sb("sum1", P, NH1)
        inv1 = sb("inv1", P, NH1)
        ao = sb("ao", P, NT, NH1, DH1)
        aoT = sb("aoT", P, S)
        y3 = sb("y3", P, NT, D)
        x3 = sb("x3", P, NT, D)
        x3T = sb("x3T", P, S)
        hid1 = sb("hid1", P, E, M1, S)
        y4 = sb("y4", P, NT, D)
        x4 = sb("x4", P, NT, D)
        logits = [sb(f"logits{i}", P, NT, E) for i in range(2)]
        top8 = [sb(f"top8_{i}", P, NT, 8) for i in range(2)]
        top2 = [sb(f"top2_{i}", P, NT, 8) for i in range(2)]
        marked = [sb(f"marked{i}", P, NT, E) for i in range(2)]
        shifted = [sb(f"shifted{i}", P, NT, E) for i in range(2)]
        rexp = [sb(f"rexp{i}", P, NT, E) for i in range(2)]
        rsum = [sb(f"rsum{i}", P, NT) for i in range(2)]
        gates = [sb(f"gates{i}", P, NT, E + 1) for i in range(2)]
        gates0T = sb("gates0T", E + 1, S)
        stats = [sb(f"stats{i}", P, NT, 6) for i in range(4)]
        mv = [sb(f"mv{i}", P, NT, 2) for i in range(4)]
        var_eps = [sb(f"var_eps{i}", P, NT) for i in range(4)]
        std_inv = [sb(f"std_inv{i}", P, NT) for i in range(4)]

        banks = {}
        for n in BANKS:
            t = ctx.enter_context(nc.psum_tensor(f"bank_{n}", [P, 512], F32))
            banks[n] = (t, sem(f"filled_{n}"), sem(f"drained_{n}"))

        loaded = [sem(f"loaded{i}") for i in range(4)]
        consts_ready = sem("consts_ready")
        wq_scaled = sem("wq_scaled")
        x_loaded = sem("x_loaded")
        sq_ready = sem("sq_ready")
        rms_ready = sem("rms_ready")
        h_ready = sem("h_ready")
        xplus_ready = sem("xplus_ready")
        probs_ready = sem("probs_ready")
        max_ready = sem("max_ready")
        stats_ready = [sem(f"stats_ready{i}") for i in range(4)]
        std_ready = [sem(f"std_ready{i}") for i in range(4)]
        ln_ready = [sem(f"ln_ready{i}") for i in range(4)]
        shifted_ready = [sem(f"shifted_ready{i}") for i in range(2)]
        rexp_ready = [sem(f"rexp_ready{i}") for i in range(2)]
        gates_ready = sem("gates_ready")
        x2plus_ready = sem("x2plus_ready")
        score_ready = sem("score_ready")
        exp1_ready = sem("exp1_ready")
        prod_ready = sem("prod_ready")
        pv1_ready = sem("pv1_ready")
        ao_ready = sem("ao_ready")
        stored = sem("stored")

        def run(eng, body, before=None):
            if before:
                before(Before(banks))
            for it in range(FIRST):
                body(Iteration(it, 0, banks))
            with eng.Fori(0, LAST - FIRST + 1) as step:
                body(Iteration(FIRST, step, banks))
            for it in range(LAST + 1, ROWS + 2):
                body(Iteration(it, 0, banks))

        def settled(eng, step):
            eng.drain()

        def head_pairs(t, hs):
            full = [P, hs.stop - hs.start, NH1, DH1]
            return (qkv1[:, t, hs, 0, :].rearrange("p h (a d) -> p h a d", a=1).broadcast_to(full),
                    qkv1[:, t, :, 1, :].rearrange("p (a g) d -> p a g d", a=1).broadcast_to(full))

        n_loads = [0] * 4

        def wait_weights(eng, v, group):
            first = {0: -1, 1: 0, 2: 1, 3: 1}[group]
            if v.it == first:
                eng.wait_ge(loaded[group], n_loads[group])
        block = ctx.enter_context(nc.Block())

        @block.sync
        def _(sp):
            def load(group, dst, src):
                sp.dma_start(dst, src).then_inc(loaded[group], 16)
                n_loads[group] += 16

            def load_x(row):
                sp.dma_start(x_row[:], x_in[row, :, :].rearrange("(t p) d -> p t d", p=P)).then_inc(x_loaded, 16)

            def replicate(src, n):
                return bass.AP(src.tensor, src.offset, [[0, P], [1, n]])

            load_x(0)
            sp.dma_start(nscale[:], norm_scale.rearrange("(p a) -> p a", a=1)).then_inc(stored, 16)
            for dst, src in ((wq, wq_in), (wk, wk_in), (wv, wv_in)):
                load(0, dst[:], src.rearrange("d h e -> d (h e)"))
            load(0, b_out[:, 0, :], replicate(b_out_in, D))
            load(1, wo[:], wo_in.rearrange("h e d -> (h e) d").rearrange("(s p) d -> p s d", p=P))
            load(1, router0_b[:, 0, :], replicate(router0_b_in, E))
            load(1, router0[:], router0_in)
            load(1, up0_b[:, 0:E, :], rb1_in)
            load(1, up0_b[:, E, :], sb1_in)
            load(1, up0[:, 0:E, :], rw1_in.rearrange("e d h -> d e h"))
            load(1, up0[:, E, :], sw1_in)
            load(2, down0[:, 0:E, :, :].rearrange("p e k d -> p (e k) d"), rw2_in.rearrange("e h d -> (e h) d").rearrange("(k p) d -> p k d", p=P))
            load(2, down0[:, E, :, :], sw2_in.rearrange("(k p) d -> p k d", p=P))
            load(2, down0_b[0:E, :], rb2_in)
            load(2, down0_b[E:E + 1, :], sb2_in.rearrange("(a d) -> a d", a=1))
            load(2, bproj[:, 0, :], replicate(bproj_in, D))
            load(2, wqkv1[:], wqkv1_in)
            load(2, wproj[:], wproj_in)
            load(3, router1[:], router1_in)
            load(3, up1[:], w1_in)
            load(3, down1[:], w2_in)

            def body(v):
                if v.next:
                    sp.wait_ge(h_ready, v.at(0, 1, 1))
                    sp.wait_ge(xplus_ready, v.at(0, 1, 1))
                    load_x(v.it + 1 + v.step)
                if v.c:
                    sp.wait_ge(ln_ready[3], v.at(2, 1, 1))
                    sp.dma_start(out[v.it - 2 + v.step, :, :].rearrange("(t p) d -> p t d", p=P), x4[:]).then_inc(stored, 16)

            run(sp, body)
            sp.wait_ge(stored, 16 * (ROWS + 1))

        @block.gpsimd
        def _(pool):
            g = nc.gpsimd
            g.memset(ident[:], 0.0).then_inc(consts_ready, 1)
            pool.wait_ge(consts_ready, 1)
            g.affine_select(out=ident[:], in_=ident[:], compare_op=ALU.not_equal, fill=1.0, base=0,
                            pattern=[[-1, P]], channel_multiplier=1)
            g.memset(minus_half[:], -0.5)
            for i in range(2):
                g.memset(top2[i][:], -3.0e38)
                g.memset(gates[i][:, :, E:E + 1], 1.0)
            g.memset(ln_eps[:], LN_EPS)
            g.memset(rms_eps[:], RMS_EPS)
            g.memset(one_over_d[:], 1.0 / D).then_inc(consts_ready, 1)
            pool.wait_ge(consts_ready, 2)
            pool.wait_ge(loaded[0], n_loads[0])

            def inverse_std(v, i, lag):
                pool.wait_ge(stats_ready[i], v.at(lag, 1, 1))
                settled(pool, g.tensor_tensor(var_eps[i][:], mv[i][:, :, 1], ln_eps[:], ALU.add))
                g.tensor_tensor(std_inv[i][:], var_eps[i][:], minus_half[:], ALU.pow).then_inc(std_ready[i], 1)

            def rms(v):
                pool.wait_ge(sq_ready, v.at(-1, 1, 1))
                settled(pool, g.tensor_tensor(mean_sq[:], sum_sq[:], one_over_d[:], ALU.mult))
                settled(pool, g.tensor_tensor(mean_sq[:], mean_sq[:], rms_eps[:], ALU.add))
                g.tensor_tensor(rms_inv[:], mean_sq[:], minus_half[:], ALU.pow).then_inc(rms_ready, 1)

            def plus(v):
                pool.wait_ge(x_loaded, v.at(-1, 16, 16))
                if v.a:
                    pool.wait_ge(*v.drain("OUT"))
                g.tensor_tensor(x_plus[:], x_row[:], b_out[:, 0:1, :].broadcast_to([P, NT, D]), ALU.add).then_inc(xplus_ready, 1)

            def head_product(v):
                pool.wait_ge(*v.drain("LQ1"))
                for half in range(2):
                    hs = slice(half * 8, half * 8 + 8)
                    q, k = head_pairs(1, hs)
                    ins = g.tensor_tensor(prod[:, 1, hs], q, k, ALU.mult)
                ins.then_inc(prod_ready, 1)

            def value_product(v, t):
                pool.wait_ge(exp1_ready, v.at(1, NT, t + 1))
                for half in range(2):
                    hs = slice(half * 8, half * 8 + 8)
                    ins = g.tensor_tensor(
                        pv1[:, t, hs], exp1[:, t, hs].rearrange("p h (a g) -> p h a g", a=1).broadcast_to([P, 8, DH1, NH1]),
                        qkv1[:, t, :, 2, :].rearrange("p g (a d) -> p a d g", a=1).broadcast_to([P, 8, DH1, NH1]), ALU.mult)
                ins.then_inc(pv1_ready, 1)

            def body(v):
                if v.b:
                    wait_weights(pool, v, 2)
                    inverse_std(v, 1, 1)
                    pool.wait_ge(ln_ready[1], v.at(1, 1, 1))
                    g.tensor_tensor(x2_plus[:], x2[:], bproj[:, 0:1, :].broadcast_to([P, NT, D]), ALU.add).then_inc(x2plus_ready, 1)
                    head_product(v)
                    value_product(v, 0)
                    value_product(v, 1)
                if v.a:
                    inverse_std(v, 0, 0)
                if v.c:
                    inverse_std(v, 3, 2)
                if v.b:
                    inverse_std(v, 2, 1)
                if v.next:
                    rms(v)
                    plus(v)

            def before(v):
                rms(v)
                plus(v)

            run(pool, body, before)

        @block.scalar
        def _(act):
            sc = nc.scalar
            act.wait_ge(consts_ready, 2)
            act.wait_ge(loaded[0], n_loads[0])
            sc.activation(wq[:], wq[:], ACT.Copy, scale=float(DH) ** -0.5).then_inc(wq_scaled, 1)

            def squares_of(v):
                act.wait_ge(x_loaded, v.at(-1, 16, 16))
                for t in range(NT):
                    ins = sc.activation(squares[:, t, :], x_row[:, t, :], ACT.Square, accum_out=sum_sq[:, t:t + 1])
                ins.then_inc(sq_ready, 1)

            def copy_out(v, name, dst, src):
                act.wait_ge(*v.fill(name))
                sc.activation(dst, src, ACT.Copy).then_inc(v.drain(name)[0], 1)

            def v_out(v, n):
                t, half = n // 2, n % 2
                copy_out(v, f"V{n}", values[:, t, half * 512:half * 512 + 512], v.bank(f"V{n}")[:, :])

            def o_out(v, s):
                copy_out(v, f"O{s}", oT[:, s, :], v.bank(f"O{s}")[:, 0:S])

            def qk_out(v, s):
                copy_out(v, f"QK{s}", qk[:, s % 2], v.bank(f"QK{s}")[:, :].rearrange("p (a n) -> p a n", a=2))

            def softmax_exp(v, h):
                act.wait_ge(max_ready, v.at(0, H, h + 1))
                for t in range(NT):
                    ins = sc.activation(probs[:, h // 2 % 2, h % 2, t, :], v.bank(f"S{h}")[:, t * S:(t + 1) * S], ACT.Exp,
                                        bias=neg_max[:, h, t:t + 1],
                                        accum_out=row_sum[:, h // 2 % 2, h % 2 * NT + t:h % 2 * NT + t + 1])
                ins.then_inc(v.drain(f"S{h}")[0], 1)

            def probsT_out(v, h):
                copy_out(v, f"T{h}", probsT[:, h % 2], v.bank(f"T{h}")[:, :].rearrange("p (k q) -> p k q", k=NT))

            def router_exp(v, i):
                lag = i + 1
                act.wait_ge(shifted_ready[i], v.at(lag, 1, 1))
                sc.activation(rexp[i][:], shifted[i][:], ACT.Exp).then_inc(rexp_ready[i], 1)

            def head_exp(v, t):
                act.wait_ge(score_ready, v.at(1, NT, t + 1))
                sc.activation(exp1[:, t], score1[:, t], ACT.Exp, scale=1.0 / 8.0).then_inc(exp1_ready, 1)

            def gelu0(v, u):
                act.wait_ge(*v.fill(f"U0_{u}"))
                for m in range(M0):
                    ins = sc.activation(hid0[:, u, m, :], v.bank(f"U0_{u}")[:, m * S:(m + 1) * S], ACT.Gelu,
                                        bias=up0_b[:, u, m:m + 1])
                ins.then_inc(v.drain(f"U0_{u}")[0], 1)

            def gelu1(v, u):
                act.wait_ge(*v.fill(f"U1_{u}"))
                e, m = u // 2, u % 2 * 2
                sc.activation(hid1[:, e, m:m + 2, :], v.bank(f"U1_{u}")[:, :].rearrange("p (m n) -> p m n", m=2),
                              ACT.Gelu).then_inc(v.drain(f"U1_{u}")[0], 1)

            def fill_out(v, s, place):
                for name in fill_units(v.it, s, place):
                    if name == "X2T":
                        copy_out(v, name, x2T[:], v.bank(name)[:, 0:S])
                    if name in ("LQ0", "LQ1"):
                        copy_out(v, name, qkv1[:, int(name[2])].rearrange("p h c d -> p (h c d)"), v.bank(name)[:, 0:3 * D])

            def body(v):
                if v.a:
                    qk_out(v, 0)
                if v.b:
                    router_exp(v, 0)
                if v.c:
                    router_exp(v, 1)
                if v.a:
                    v_out(v, 0)
                    qk_out(v, 1)
                    softmax_exp(v, 0)
                    softmax_exp(v, 1)
                    v_out(v, 2)
                for s in range(HP):
                    if v.a and s + 1 < HP:
                        softmax_exp(v, 2 * s + 2)
                        softmax_exp(v, 2 * s + 3)
                    if v.a and s >= 1:
                        o_out(v, s - 1)
                    fill_out(v, s, 0)
                    if v.a:
                        probsT_out(v, 2 * s)
                        probsT_out(v, 2 * s + 1)
                        if s + 2 < HP:
                            qk_out(v, s + 2)
                    fill_out(v, s, 1)
                    if v.b and s in (5, 6):
                        head_exp(v, s - 5)
                if v.a:
                    o_out(v, HP - 1)
                if v.a:
                    wait_weights(act, v, 1)
                    for u in range(E + 1):
                        gelu0(v, u)
                if v.next:
                    squares_of(v)
                if v.b:
                    for u in range(2 * E):
                        gelu1(v, u)

            run(act, body, squares_of)

        @block.vector
        def _(dve):
            ve = nc.vector
            dve.wait_ge(stored, 16)
            dve.wait_ge(consts_ready, 2)

            def head_max(v, h):
                dve.wait_ge(*v.fill(f"S{h}"))
                ve.tensor_reduce(neg_max[:, h, :], v.bank(f"S{h}")[:, :].rearrange("p (t k) -> p t k", t=NT),
                                 AX.X, ALU.max, negate=True).then_inc(max_ready, 1)

            def normalise(v, s):
                for j in range(2):
                    dve.wait_ge(*v.drain(f"S{2 * s + j}"))
                settled(dve, ve.reciprocal(row_inv[:, s % 2, :], row_sum[:, s % 2, :]))
                for j in range(2):
                    for t in range(NT):
                        n = j * NT + t
                        ins = ve.tensor_scalar(probs[:, s % 2, j, t, :], probs[:, s % 2, j, t, :], row_inv[:, s % 2, n:n + 1],
                                               None, ALU.mult)
                    ins.then_inc(probs_ready, 1)

            def v_out(v, n):
                dve.wait_ge(*v.fill(f"V{n}"))
                ve.tensor_copy(values[:, n // 2, n % 2 * 512:n % 2 * 512 + 512], v.bank(f"V{n}")[:, :]).then_inc(v.drain(f"V{n}")[0], 1)

            def ln_stats(v, i, y, lag):
                for t in range(NT):
                    settled(dve, ve.bn_stats(stats[i][:, t, :], y[:, t, :]))
                for t in range(NT):
                    ins = ve.bn_aggr(mv[i][:, t, :], stats[i][:, t, :])
                ins.then_inc(stats_ready[i], 1)

            def ln_apply(v, i, y, dst, lag):
                dve.wait_ge(std_ready[i], v.at(lag, 1, 1))
                for t in range(NT):
                    ins = ve.tensor_scalar(dst[:, t, :], y[:, t, :], mv[i][:, t, 0:1], std_inv[i][:, t:t + 1],
                                           ALU.subtract, ALU.mult)
                ins.then_inc(ln_ready[i], 1)

            def route(v, i):
                for t in range(NT):
                    settled(dve, ve.max(top8[i][:, t, :], logits[i][:, t, :]))
                settled(dve, ve.tensor_copy(top2[i][:, :, 0:2], top8[i][:, :, 0:2]))
                for t in range(NT):
                    settled(dve, ve.match_replace(marked[i][:, t, :], top2[i][:, t, :], logits[i][:, t, :], -3.0e38))
                ve.tensor_tensor(shifted[i][:], logits[i][:], top8[i][:, :, 0:1].broadcast_to([P, NT, E]),
                                 ALU.subtract).then_inc(shifted_ready[i], 1)
                settled(dve, ve.tensor_tensor(marked[i][:], marked[i][:], logits[i][:], ALU.not_equal))

            def gate(v, i, lag):
                dve.wait_ge(rexp_ready[i], v.at(lag, 1, 1))
                settled(dve, ve.reduce_sum(rsum[i][:], rexp[i][:], AX.X))
                settled(dve, ve.reciprocal(rsum[i][:], rsum[i][:]))
                settled(dve, ve.tensor_tensor(marked[i][:], marked[i][:], rexp[i][:], ALU.mult))
                ins = ve.tensor_tensor(gates[i][:, :, 0:E], marked[i][:], rsum[i][:].rearrange("p (t a) -> p t a", a=1).broadcast_to([P, NT, E]),
                                       ALU.mult)
                if i == 0:
                    ins.then_inc(gates_ready, 1)
                settled(dve, ins)

            def mix(v, name, i, experts, acc, first):
                dve.wait_ge(*v.fill(name))
                y = v.bank(name)[:, 0:len(experts) * NT * D].rearrange("p (j t d) -> p j t d", j=len(experts), t=NT)
                for j, e in enumerate(experts):
                    src = first if e == 0 else acc
                    for t in range(NT):
                        ins = ve.scalar_tensor_tensor(acc[:, t, :], y[:, j, t, :], gates[i][:, t, e:e + 1], src[:, t, :],
                                                      ALU.mult, ALU.add)
                    if e == experts[-1]:
                        ins.then_inc(v.drain(name)[0], 1)
                    settled(dve, ins)

            def head_product(v):
                dve.wait_ge(*v.drain("LQ0"))
                q, k = head_pairs(0, slice(0, NH1))
                settled(dve, ve.tensor_tensor(prod[:, 0], q, k, ALU.mult))

            def head_scores(v, t):
                if t == 1:
                    dve.wait_ge(prod_ready, v.at(1, 1, 1))
                settled(dve, ve.reduce_sum(score1[:, t], prod[:, t], AX.X))
                settled(dve, ve.reduce_max(max1[:], score1[:, t], AX.X))
                ve.tensor_tensor(score1[:, t], score1[:, t], max1[:].rearrange("p (h a) -> p h a", a=1).broadcast_to([P, NH1, NH1]),
                                 ALU.subtract).then_inc(score_ready, 1)

            def head_mix(v, t):
                dve.wait_ge(exp1_ready, v.at(1, NT, t + 1))
                settled(dve, ve.reduce_sum(sum1[:], exp1[:, t], AX.X))
                settled(dve, ve.reciprocal(inv1[:], sum1[:]))
                dve.wait_ge(pv1_ready, v.at(1, NT, t + 1))
                settled(dve, ve.reduce_sum(ao[:, t], pv1[:, t], AX.X))
                ve.tensor_tensor(ao[:, t], ao[:, t], inv1[:].rearrange("p (h a) -> p h a", a=1).broadcast_to([P, NH1, DH1]),
                                 ALU.mult).then_inc(ao_ready, 1)

            def input_norm(v):
                dve.wait_ge(rms_ready, v.at(-1, 1, 1))
                dve.wait_ge(x_loaded, v.at(-1, 16, 16))
                for t in range(NT):
                    ins = ve.tensor_scalar(h_row[:, t, :], x_row[:, t, :], rms_inv[:, t:t + 1], None, ALU.mult)
                ins.then_inc(h_ready, 1)
                dve.wait_ge(*v.fill("HT"))
                ve.tensor_scalar(hT[:], v.bank("HT")[:, 0:S], nscale[:, 0:1], None, ALU.mult).then_inc(v.drain("HT")[0], 1)

            def residual(v, name, y, x):
                dve.wait_ge(*v.fill(name))
                ve.tensor_tensor(y[:], v.bank(name)[:, 0:NT * D].rearrange("p (t d) -> p t d", t=NT),
                                 x[:], ALU.add).then_inc(v.drain(name)[0], 1)
                dve.drain()

            def transposed_out(v, name, xT):
                dve.wait_ge(*v.fill(name))
                ve.tensor_copy(xT[:], v.bank(name)[:, 0:S]).then_inc(v.drain(name)[0], 1)

            def fill_out(v, s, place):
                for name in fill_units(v.it, s, place):
                    if name == "WT0":
                        dve.wait_ge(*v.fill("WT0"))
                        ve.tensor_copy(gates0T[:], v.bank("WT0")[0:E + 1, 0:S]).then_inc(v.drain("WT0")[0], 1)
                    if name[:3] == "D0p":
                        p = int(name[3:])
                        mix(v, name, 0, (2 * p, 2 * p + 1), y2, x1)
                    if name == "D0base":
                        residual(v, name, y2, y2)
                        ln_stats(v, 1, y2, 1)
                    if name[:3] == "D1e":
                        mix(v, name, 1, (int(name[3:]),), y4, x3)

            def body(v):
                if v.a:
                    head_max(v, 0)
                    head_max(v, 1)
                    v_out(v, 1)
                if v.b:
                    gate(v, 0, 1)
                if v.a:
                    v_out(v, 3)
                    normalise(v, 0)
                if v.c:
                    gate(v, 1, 2)
                for s in range(HP):
                    if v.a and s + 1 < HP:
                        head_max(v, 2 * s + 2)
                        head_max(v, 2 * s + 3)
                    if v.b and s == 3:
                        ln_apply(v, 1, y2, x2, 1)
                    fill_out(v, s, 0)
                    if v.b and s == 4:
                        head_product(v)
                    if v.b and s in (5, 6):
                        head_scores(v, s - 5)
                    if v.a and s + 1 < HP:
                        normalise(v, s + 1)
                    if v.b and s == 7:
                        head_mix(v, 0)
                    fill_out(v, s, 1)
                if v.a:
                    dve.wait_ge(xplus_ready, v.at(0, 1, 1))
                    residual(v, "OUT", y1, x_plus)
                    ln_stats(v, 0, y1, 0)
                if v.c:
                    mix(v, "D1e6", 1, (6,), y4, x3)
                if v.a:
                    ln_apply(v, 0, y1, x1, 0)
                if v.c:
                    mix(v, "D1e7", 1, (7,), y4, x3)
                if v.a:
                    transposed_out(v, "X1T", x1T)
                if v.c:
                    ln_stats(v, 3, y4, 2)
                if v.b:
                    head_mix(v, 1)
                if v.a:
                    wait_weights(dve, v, 1)
                    dve.wait_ge(*v.fill("R0"))
                    ve.tensor_tensor(logits[0][:], v.bank("R0")[:, 0:NT * E].rearrange("p (t e) -> p t e", t=NT),
                                     router0_b[:, 0:1, :].broadcast_to([P, NT, E]), ALU.add).then_inc(v.drain("R0")[0], 1)
                    dve.drain()
                if v.c:
                    dve.wait_ge(stored, v.at(2, 16, 16))
                    ln_apply(v, 3, y4, x4, 2)
                if v.b:
                    transposed_out(v, "AOT", aoT)
                    dve.wait_ge(x2plus_ready, v.at(1, 1, 1))
                    residual(v, "PROJ", y3, x2_plus)
                    ln_stats(v, 2, y3, 1)
                if v.a:
                    route(v, 0)
                if v.b:
                    ln_apply(v, 2, y3, x3, 1)
                    transposed_out(v, "X3T", x3T)
                    dve.wait_ge(*v.fill("R1"))
                    ve.tensor_copy(logits[1][:], v.bank("R1")[:, 0:NT * E].rearrange("p (t e) -> p t e", t=NT)).then_inc(v.drain("R1")[0], 1)
                    dve.drain()
                    route(v, 1)
                if v.next:
                    input_norm(v)

            run(dve, body, input_norm)

        @block.tensor
        def _(pe):
            te = nc.tensor
            pe.wait_ge(consts_ready, 2)

            def tokens(t):
                return slice(t * P, (t + 1) * P)

            def transpose_row(bank, src):
                for t in range(NT):
                    ins = te.transpose(bank[0:src.shape[2], tokens(t)], src[:, t, :], ident[:])
                return ins

            def wait_drained(v, name, source):
                if v.nth[source][0] != v.nth[name][0]:
                    pe.wait_ge(*v.drain(source))

            def unit(v, name):
                bank = v.bank(name)

                if name[0] == "V":
                    n = int(name[1:])
                    return te.matmul(bank[:, :], hT[:, tokens(n // 2)], wv[:, n % 2 * 512:n % 2 * 512 + 512], start=True, stop=True)
                if name[:2] == "QK":
                    s = int(name[2:])
                    if s == 0:
                        pe.wait_ge(*drained_ht(v))
                        if v.it == 0:
                            pe.wait_ge(loaded[0], n_loads[0])
                            pe.wait_ge(wq_scaled, 1)
                    te.matmul(bank[:, 0:S], wq[:, tokens(s)], hT[:], start=True, stop=True)
                    return te.matmul(bank[:, S:2 * S], wk[:, tokens(s)], hT[:], start=True, stop=True)
                if name[0] == "S":
                    h = int(name[1:])
                    s, r = h // 2, slice(h % 2 * DH, h % 2 * DH + DH)
                    wait_drained(v, name, f"QK{s}")
                    for t in range(NT):
                        ins = te.matmul(bank[:, t * S:(t + 1) * S], qk[r, s % 2, 0, tokens(t)], qk[r, s % 2, 1, :], start=True, stop=True)
                    return ins
                if name[0] == "T":
                    h = int(name[1:])
                    pe.wait_ge(probs_ready, v.at(0, H, h + 1))
                    for k in range(NT):
                        for t in range(NT):
                            ins = te.transpose(bank[:, k * S + t * P:k * S + (t + 1) * P], probs[:, h // 2 % 2, h % 2, t, tokens(k)], ident[:])
                    return ins
                if name == "OUT":
                    wait_weights(pe, v, 1)
                if name == "D0p0":
                    wait_weights(pe, v, 2)
                if name == "X3T":
                    wait_weights(pe, v, 3)
                if name == "OUT":
                    for t in range(NT):
                        for s in range(HP):
                            if t == 0 and s == HP - 1:
                                wait_drained(v, name, f"O{s}")
                            ins = te.matmul(bank[:, tokens(t)], oT[:, s, tokens(t)], wo[:, s, :], start=s == 0, stop=s == HP - 1)
                    return ins
                if name[0] == "O":
                    s = int(name[1:])
                    if s == 0:
                        for n in range(2, 4):
                            wait_drained(v, name, f"V{n}")
                    for j in range(2):
                        pe.wait_ge(*v.drain(f"T{2 * s + j}"))
                    for k in range(NT):
                        for j in range(2):
                            r = slice(j * DH, j * DH + DH)
                            ins = te.matmul(bank[r, 0:S], values[:, k, s * P + j * DH:s * P + j * DH + DH],
                                            probsT[:, j, k, :], start=k == 0, stop=k == NT - 1)
                    return ins
                if name == "X1T":
                    pe.wait_ge(ln_ready[0], v.at(0, 1, 1))
                    return transpose_row(bank, x1)
                if name == "X2T":
                    pe.wait_ge(ln_ready[1], v.at(1, 1, 1))
                    return transpose_row(bank, x2)
                if name == "X3T":
                    pe.wait_ge(ln_ready[2], v.at(1, 1, 1))
                    return transpose_row(bank, x3)
                if name == "HT":
                    pe.wait_ge(h_ready, v.at(-1, 1, 1))
                    return transpose_row(bank, h_row)
                if name in ("R0", "R1"):
                    xT, w = ((x1T, router0), (x3T, router1))[int(name[1])]
                    for t in range(NT):
                        ins = te.matmul(bank[:, t * E:(t + 1) * E], xT[:, tokens(t)], w[:], start=True, stop=True)
                    return ins
                if name == "WT0":
                    pe.wait_ge(gates_ready, v.at(1, 1, 1))
                    return transpose_row(bank, gates[0])
                if name[:3] == "U0_":
                    e = int(name[3:])
                    if e == 0:
                        wait_drained(v, name, "X1T")
                    for m in range(M0):
                        ins = te.matmul(bank[:, m * S:(m + 1) * S], up0[:, e, tokens(m)], x1T[:], start=True, stop=True)
                    return ins
                if name[:3] == "U1_":
                    u = int(name[3:])
                    if u == 0:
                        wait_drained(v, name, "X3T")
                    for m in range(2):
                        ins = te.matmul(bank[:, m * S:(m + 1) * S], up1[:, u // 2, tokens(u % 2 * 2 + m)], x3T[:], start=True, stop=True)
                    return ins
                if name == "D0base":
                    wait_drained(v, name, "WT0")
                    for t in range(NT):
                        for k in range(M0):
                            te.matmul(bank[:, tokens(t)], hid0[:, E, k, tokens(t)], down0[:, E, k, :], start=k == 0, stop=False)
                        ins = te.matmul(bank[:, tokens(t)], gates0T[:, tokens(t)], down0_b[:], start=False, stop=True)
                    return ins
                if name[:3] in ("D0p", "D1e"):
                    hid, down, m, n = ((hid0, down0, M0, 2), (hid1, down1, M1, 1))[int(name[1])]
                    for j in range(n):
                        e = n * int(name[3:]) + j
                        for t in range(NT):
                            for k in range(m):
                                ins = te.matmul(bank[:, (j * NT + t) * P:(j * NT + t + 1) * P], hid[:, e, k, tokens(t)],
                                                down[:, e, k, :], start=k == 0, stop=k == m - 1)
                    return ins
                if name in ("LQ0", "LQ1"):
                    t = int(name[2])
                    wait_drained(v, name, "X2T")
                    return te.matmul(bank[:, 0:3 * D], x2T[:, tokens(t)], wqkv1[:], start=True, stop=True)
                if name == "AOT":
                    pe.wait_ge(ao_ready, v.at(1, NT, NT))
                    return transpose_row(bank, ao[:].rearrange("p t h d -> p t (h d)"))
                assert name == "PROJ"
                wait_drained(v, name, "AOT")
                for t in range(NT):
                    ins = te.matmul(bank[:, tokens(t)], aoT[:, tokens(t)], wproj[:], start=True, stop=True)
                return ins

            def drained_ht(v):
                if v.it == 0:
                    return banks["A0"][2], 1
                bank, n = Iteration(v.it - 1, v.step, banks).nth["HT"]
                return banks[bank][2], n + v.step * v.per[bank]

            def body(v):
                for name, bank in (pe_units(v.it) if v.it >= 0 else PRE):
                    free, count = v.drain(name, before=1)
                    if v.it > 0 or count:
                        pe.wait_ge(free, count)
                    unit(v, name).then_inc(v.fill(name)[0], 1)

            run(pe, body, body)


def kernel(**inputs):
    import numpy as np
    import concourse.bacc as bacc
    from concourse import mybir as mb
    from concourse.bass_utils import run_bass_kernel_spmd

    i = {k: np.asarray(v) for k, v in inputs.items()}
    E_, H0, H1 = 8, 256, 512
    arrays = {
        "x": i["L0_attn_x"], "norm_scale": i["L0_attn_norm_scale"], "wq": i["L0_attn_wq"], "wk": i["L0_attn_wk"],
        "wv": i["L0_attn_wv"], "wo": i["L0_attn_w_out"], "b_out": i["L0_attn_b_out"],
        "router0": i["L0_ffn_router_w"], "router0_b": i["L0_ffn_router_b"], "sw1": i["L0_ffn_sw1"],
        "sb1": i["L0_ffn_sb1"].reshape(H0 // 128, 128).transpose(1, 0), "sw2": i["L0_ffn_sw2"], "sb2": i["L0_ffn_sb2"],
        "rw1": i["L0_ffn_rw1"], "rb1": i["L0_ffn_rb1"].reshape(E_, H0 // 128, 128).transpose(2, 0, 1),
        "rw2": i["L0_ffn_rw2"], "rb2": i["L0_ffn_rb2"],
        "wqkv1": i["L1_attn_Wqkv"].transpose(1, 0), "wproj": i["L1_attn_Wproj"].transpose(1, 0), "bproj": i["L1_attn_bproj"],
        "router1": i["L1_ffn_router_w"].transpose(1, 0), "w1": i["L1_ffn_w1"].transpose(2, 0, 1),
        "w2": i["L1_ffn_w2"].reshape(E_, 128, H1 // 128, 128).transpose(3, 0, 2, 1),
    }
    arrays = {f"in_{k}": np.ascontiguousarray(v) for k, v in arrays.items()}
    nc = bacc.Bacc("TRN2", target_bir_lowering=False, num_devices=1)
    args = [nc.dram_tensor(k, v.shape, mb.dt.from_np(v.dtype), kind="ExternalInput").ap() for k, v in arrays.items()]
    out = nc.dram_tensor("out", (16, 256, 128), mb.dt.from_np(np.dtype("float32")), kind="ExternalOutput").ap()
    transformer_blocks(nc, *args, out)
    r = run_bass_kernel_spmd(nc, [arrays], core_ids=[0])
    return r.results[0]["out"]
```

```python
import concourse.bass as bass
from concourse import mybir
from contextlib import ExitStack

F32 = mybir.dt.float32
F32R = mybir.dt.float32r
ALU = mybir.AluOpType
ACT = mybir.ActivationFunctionType
AX = mybir.AxisListType

P = 128
ROWS, S, D = 16, 256, 128
NT = S // P
H, DH = 16, 64
HP = H // 2
E = 8
HID0, HID1 = 256, 512
M0, M1 = HID0 // P, HID1 // P
NH1, DH1 = 16, 8
SCALE = float(DH) ** -0.5
LN_EPS, RMS_EPS = 1e-5, 1e-6
SPLIT1 = 6
FIRST, LAST = 2, ROWS - 2



FILL_B = {(0, 1): ["D0p2"], (1, 0): ["WT0"], (1, 1): ["D0p3"], (2, 0): ["D0base"], (3, 0): ["X2T"], (3, 1): ["LQ0", "LQ1"]}
FILL_C = {(2, 1): ["D1e0"], (4, 1): ["D1e1"], (5, 1): ["D1e2"], (6, 1): ["D1e3"], (7, 0): ["D1e4"], (7, 1): ["D1e5"]}


def fill_units(it, s, place):
    b, c = 1 <= it <= ROWS, 2 <= it <= ROWS + 1
    return (FILL_B.get((s, place), []) if b else []) + (FILL_C.get((s, place), []) if c else [])


def pe_units(it):
    a, b, c, nxt = it < ROWS, 1 <= it <= ROWS, 2 <= it <= ROWS + 1, it < ROWS - 1
    order = []
    rings = {"A": ["A0", "A1"], "F": ["F0", "F1"], "G": ["F0", "F1", "T0", "T1"]}
    turn = {"A": 0, "F": 0, "G": 1}

    def put(ring, *names, on=True):
        for name in names if on else ():
            banks = rings.get(ring, [ring])
            order.append((name, banks[turn.get(ring, 0) % len(banks)]))
            if ring in turn:
                turn[ring] += 1

    put("F", "D0p0", "D0p1", on=b)
    for s in range(HP):
        put("S0", f"S{2 * s + 2}", on=a and s + 1 < HP)
        put("S1", f"S{2 * s + 3}", on=a and s + 1 < HP)
        put("A", "QK2", on=a and s == 0)
        put("A", f"O{s - 1}", on=a and s >= 1)
        put("F", *fill_units(it, s, 0))
        put("T0", f"T{2 * s}", on=a)
        put("T1", f"T{2 * s + 1}", on=a)
        put("A", f"QK{s + 3}", on=a and s + 3 < HP)
        put("A", "HT", on=nxt and s == HP - 2)
        put("F", *fill_units(it, s, 1))
    put("A", f"O{HP - 1}", "OUT", on=a)
    put("F", "D1e6", "D1e7", on=c)
    put("A", "V0", on=nxt)
    put("A", "X1T", on=a)
    put("G", "V1", on=nxt)
    put("A", "V2", on=nxt)
    put("G", "U0_0", "U0_1", on=a)
    put("A", "R0", on=a)
    put("G", "U0_2", "U0_3", on=a)
    put("G", "AOT", on=b)
    put("G", "U0_4", on=a)
    put("G", "PROJ", on=b)
    put("G", "U0_5", "U0_6", "U0_7", "U0_8", on=a)
    put("A", "V3", on=nxt)
    put("G", "X3T", on=b)
    put("A", "QK0", "QK1", on=nxt)
    put("G", "U1_0", "U1_1", "U1_2", "R1", "U1_3", "U1_4", on=b)
    put("G", "U1_5", "U1_6", on=b)
    put("S0", "S0", on=nxt)
    put("S1", "S1", on=nxt)
    put("G", *[f"U1_{u}" for u in range(7, 2 * E)], on=b)
    return order


PRE = [("HT", "A0"), ("V0", "A1"), ("V1", "A0"), ("V2", "A1"), ("V3", "A0"), ("QK0", "A1"), ("QK1", "A0"), ("S0", "S0"), ("S1", "S1")]
BANKS = ["S0", "S1", "T0", "T1", "A0", "A1", "F0", "F1"]


def count_units(it):
    seen = {k: 0 for k in BANKS}
    for units in [PRE] + [pe_units(i) for i in range(it)]:
        for _, bank in units:
            seen[bank] += 1
    return seen


def number_units(units, seen):
    nth, per = {}, {k: 0 for k in BANKS}
    for name, bank in units:
        per[bank] += 1
        nth[name] = (bank, seen[bank] + per[bank])
    return nth, per


class Iteration:

    def __init__(self, it, step, banks):
        self.it, self.step, self.banks = it, step, banks
        self.a, self.b, self.c = it < ROWS, 1 <= it <= ROWS, 2 <= it <= ROWS + 1
        self.next = it < ROWS - 1
        self.nth, self.per = number_units(pe_units(it), count_units(it))

    def previous(self):
        if self.it == 0:
            return Before(self.banks)
        view = Iteration(self.it - 1, self.step, self.banks)
        view.per = self.per
        return view

    def at(self, lag, per, k):
        return (self.it - lag) * per + k + self.step * per

    def fill(self, name, before=0):
        bank, n = self.nth[name]
        return self.banks[bank][1], n - before + self.step * self.per[bank]

    def drain(self, name, before=0):
        bank, n = self.nth[name]
        return self.banks[bank][2], n - before + self.step * self.per[bank]

    def bank(self, name):
        return self.banks[self.nth[name][0]][0]


class Before(Iteration):

    def __init__(self, banks):
        self.it, self.step, self.banks = -1, 0, banks
        self.a = self.b = self.c = False
        self.next = True
        self.nth, self.per = number_units(PRE, {k: 0 for k in BANKS})


def transformer_blocks(nc, x_in, norm_scale, wq_in, wk_in, wv_in, wo_in, b_out_in,
                       router0_in, router0_b_in, sw1_in, sb1_in, sw2_in, sb2_in, rw1_in, rb1_in, rw2_in,
                       rb2_in, wqkv1_in, wproj_in, bproj_in, router1_in, w1_in, w2_in, out):
    ctx = ExitStack()
    with ctx:
        def sb(name, *shape):
            return ctx.enter_context(nc.sbuf_tensor(name, list(shape), F32))

        def split(name, *shape):
            return ctx.enter_context(nc.sbuf_tensor(name, list(shape), F32R))

        def sem(name):
            return ctx.enter_context(nc.semaphore(name))

        wv, wq, wk = ((split(f"{n}_hi", P, H * DH), split(f"{n}_lo", P, H * DH)) for n in ("wv", "wq", "wk"))
        wo = sb("wo", P, HP, D)
        nscale = sb("nscale", P, 1)
        b_out = sb("b_out", P, 1, D)
        bproj = sb("bproj", P, 1, D)
        router0_in_sb = sb("router0_in_sb", P, E)
        router0 = split("router0_hi", P, E), split("router0_lo", P, E)
        router0_b = sb("router0_b", P, 1, E)
        router1 = sb("router1", P, E)
        up0 = split("up0_hi", P, E + 1, HID0), split("up0_lo", P, E + 1, HID0)
        up0_b = sb("up0_b", P, E + 1, M0)
        down0 = sb("down0", P, E + 1, M0, D)
        down0_b = sb("down0_b", E + 1, D)
        wqkv1 = sb("wqkv1", P, 3 * D)
        wproj = sb("wproj", P, D)
        up1 = split("up1_hi", P, SPLIT1, HID1), split("up1_lo", P, SPLIT1, HID1)
        up1_whole = sb("up1_whole", P, E - SPLIT1, HID1)
        down1 = sb("down1", P, E, M1, D)
        ident = sb("ident", P, P)
        table_load = sb("table_load", P, 1)
        minus_half, ln_eps, rms_eps, one_over_d = (sb(n, P, NT) for n in ("minus_half", "ln_eps", "rms_eps", "one_over_d"))

        x_row = sb("x_row", P, NT, D)
        x_plus = sb("x_plus", P, NT, D)
        sum_sq = sb("sum_sq", P, NT)
        mean_sq = sb("mean_sq", P, NT)
        rms_inv = sb("rms_inv", P, NT)
        h_row = sb("h_row", P, NT, D)
        hT = split("hT_hi", P, S), split("hT_lo", P, S)
        values = sb("values", P, NT, H * DH)
        qk_hi, qk_lo = (split(n, P, 2, 2, S) for n in ("qk_hi", "qk_lo"))
        neg_max = sb("neg_max", P, H, NT)
        probs = sb("probs", P, 2, 2, NT, S)
        probsT = sb("probsT", P, 2, NT, S)
        row_sum = sb("row_sum", P, 2, 2 * NT)
        row_inv = sb("row_inv", P, 2, 2 * NT)
        oT = sb("oT", P, HP, S)
        x1 = sb("x1", P, NT, D)
        x1T = split("x1T_hi", P, S), split("x1T_lo", P, S)
        hid0 = sb("hid0", P, E + 1, M0, S)
        x2 = sb("x2", P, NT, D)
        x2T = sb("x2T", P, S)
        gates0T = x2T[0:E + 1, :]
        aoT = x3T = x2T
        qkv1 = sb("qkv1", P, NT, NH1, 3, DH1)
        prod = hid0[:, 0:E].rearrange("p (t e) m (h g d) -> p t (e m h) g d", t=NT, h=S // (NH1 * DH1), g=NH1)
        score1 = hid0[:, E].rearrange("p m (h g) -> p m h g", g=NH1)
        max1 = sb("max1", P, NH1)
        pv1 = prod.rearrange("p t h (d x) c -> p t h d (x c)", d=DH1)
        sum1 = sb("sum1", P, NT, NH1)
        inv1 = sb("inv1", P, NT, NH1)
        ao = sb("ao", P, NT, NH1, DH1)
        x3 = sb("x3", P, NT, D)
        x3T_parts = x1T
        hid1 = sb("hid1", P, E, M1, S)
        projections = [hid1[:, n].rearrange("p m s -> p (m s)") for n in range(3)]
        up1_loaded = hid1[:, 3:6].rearrange("p e m s -> p (e m s)")[:, 0:SPLIT1 * HID1].rearrange("p (e h) -> p e h", e=SPLIT1)
        up0_loaded = hid0[:, 0:5].rearrange("p e m s -> p (e m s)")[:, 0:(E + 1) * HID0].rearrange("p (e h) -> p e h", e=E + 1)
        x4 = sb("x4", P, NT, D)
        logits = [sb(f"logits{i}", P, NT, E) for i in range(2)]
        top8 = [sb(f"top8_{i}", P, NT, 8) for i in range(2)]
        top2 = [sb(f"top2_{i}", P, NT, 8) for i in range(2)]
        marked = [sb(f"marked{i}", P, NT, E) for i in range(2)]
        shifted = [sb(f"shifted{i}", P, NT, E) for i in range(2)]
        rexp = [sb(f"rexp{i}", P, NT, E) for i in range(2)]
        rsum = [sb(f"rsum{i}", P, NT) for i in range(2)]
        gates = [sb(f"gates{i}", P, NT, E + 1) for i in range(2)]
        stats = [sb(f"stats{i}", P, NT, 6) for i in range(4)]
        mv = [sb(f"mv{i}", P, NT, 2) for i in range(4)]
        var_eps = [sb(f"var_eps{i}", P, NT) for i in range(4)]
        std_inv = [sb(f"std_inv{i}", P, NT) for i in range(4)]

        banks = {}
        for n in BANKS:
            t = ctx.enter_context(nc.psum_tensor(f"bank_{n}", [P, 512], F32))
            banks[n] = (t, sem(f"filled_{n}"), sem(f"drained_{n}"))

        loaded = [sem(f"loaded{i}") for i in range(5)]
        consts_ready = sem("consts_ready")
        weights_rounded = sem("weights_rounded")
        weights_split = sem("weights_split")
        up_split = sem("up_split")
        qk_rounded = sem("qk_rounded")
        x_loaded = sem("x_loaded")
        sq_ready = sem("sq_ready")
        rms_ready = sem("rms_ready")
        h_ready = sem("h_ready")
        xplus_ready = sem("xplus_ready")
        probs_ready = sem("probs_ready")
        max_ready = sem("max_ready")
        stats_ready = [sem(f"stats_ready{i}") for i in range(4)]
        std_ready = [sem(f"std_ready{i}") for i in range(4)]
        ln_ready = [sem(f"ln_ready{i}") for i in range(4)]
        shifted_ready = [sem(f"shifted_ready{i}") for i in range(2)]
        rexp_ready = [sem(f"rexp_ready{i}") for i in range(2)]
        gates_ready = sem("gates_ready")
        x2plus_ready = sem("x2plus_ready")
        score_ready = sem("score_ready")
        exp1_ready = sem("exp1_ready")
        prod_ready = sem("prod_ready")
        pv1_ready = sem("pv1_ready")
        ao_ready = sem("ao_ready")
        stored = sem("stored")

        def run(eng, body, before=None):
            if before:
                before(Before(banks))
            for it in range(FIRST):
                body(Iteration(it, 0, banks))
            with eng.Fori(0, LAST - FIRST + 1) as step:
                body(Iteration(FIRST, step, banks))
            for it in range(LAST + 1, ROWS + 2):
                body(Iteration(it, 0, banks))

        def settled(eng, step):
            eng.drain()

        def half(i):
            return slice(i * NH1 // 2, (i + 1) * NH1 // 2)

        def head_pairs(t, hs):
            full = [P, hs.stop - hs.start, NH1, DH1]
            return (qkv1[:, t, hs, 0, :].rearrange("p h (a d) -> p h a d", a=1).broadcast_to(full),
                    qkv1[:, t, :, 1, :].rearrange("p (a g) d -> p a g d", a=1).broadcast_to(full))

        def weights_and_values(t, i):
            full = [P, NH1 // 2, DH1, NH1]
            return (score1[:, t, half(i)].rearrange("p h (a g) -> p h a g", a=1).broadcast_to(full),
                    qkv1[:, t, :, 2, :].rearrange("p g (a d) -> p a d g", a=1).broadcast_to(full))

        n_loads = [0] * 5

        def wait_weights(eng, v, group):
            first = {0: -1, 1: -1, 2: 0, 3: 1, 4: 1}[group]
            if v.it == first:
                eng.wait_ge(loaded[group], n_loads[group])
        block = ctx.enter_context(nc.Block())

        @block.sync
        def _(sp):
            def load(group, dst, src):
                sp.dma_start(dst, src).then_inc(loaded[group], 16)
                n_loads[group] += 16

            def load_x(row):
                sp.dma_start(x_row[:], x_in[row, :, :].rearrange("(t p) d -> p t d", p=P)).then_inc(x_loaded, 16)

            def replicate(src, n):
                return bass.AP(src.tensor, src.offset, [[0, P], [1, n]])

            load_x(0)
            sp.dma_start(nscale[:], norm_scale.rearrange("(p a) -> p a", a=1)).then_inc(stored, 16)
            for group, dst, src in zip((0, 1, 1), projections, (wv_in, wq_in, wk_in)):
                load(group, dst, src.rearrange("d h e -> d (h e)"))
            load(1, b_out[:, 0, :], replicate(b_out_in, D))
            load(2, wo[:], wo_in.rearrange("h e d -> (h e) d").rearrange("(s p) d -> p s d", p=P))
            load(2, router0_b[:, 0, :], replicate(router0_b_in, E))
            load(2, router0_in_sb[:], router0_in)
            load(2, up0_b[:, 0:E, :], rb1_in)
            load(2, up0_b[:, E, :], sb1_in)
            load(2, up0_loaded[:, 0:E, :], rw1_in.rearrange("e d h -> d e h"))
            load(2, up0_loaded[:, E, :], sw1_in)
            load(3, down0[:, 0:E, :, :].rearrange("p e k d -> p (e k) d"), rw2_in.rearrange("e h d -> (e h) d").rearrange("(k p) d -> p k d", p=P))
            load(3, down0[:, E, :, :], sw2_in.rearrange("(k p) d -> p k d", p=P))
            load(3, down0_b[0:E, :], rb2_in)
            load(3, down0_b[E:E + 1, :], sb2_in.rearrange("(a d) -> a d", a=1))
            load(3, bproj[:, 0, :], replicate(bproj_in, D))
            load(3, wqkv1[:], wqkv1_in)
            load(3, wproj[:], wproj_in)
            load(4, router1[:], router1_in)
            load(4, up1_loaded, w1_in[:, 0:SPLIT1, :])
            load(4, up1_whole[:], w1_in[:, SPLIT1:E, :])
            load(4, down1[:], w2_in)

            def body(v):
                if v.next:
                    sp.wait_ge(h_ready, v.at(0, 1, 1))
                    sp.wait_ge(xplus_ready, v.at(0, 1, 1))
                    load_x(v.it + 1 + v.step)
                if v.c:
                    sp.wait_ge(ln_ready[3], v.at(2, 1, 1))
                    sp.dma_start(out[v.it - 2 + v.step, :, :].rearrange("(t p) d -> p t d", p=P), x4[:]).then_inc(stored, 16)

            run(sp, body)
            sp.wait_ge(stored, 16 * (ROWS + 1))

        @block.gpsimd
        def _(pool):
            g = nc.gpsimd
            g.memset(ident[:], 0.0).then_inc(consts_ready, 1)
            pool.wait_ge(consts_ready, 1)
            g.affine_select(out=ident[:], in_=ident[:], compare_op=ALU.not_equal, fill=1.0, base=0,
                            pattern=[[-1, P]], channel_multiplier=1)
            g.memset(minus_half[:], -0.5)
            g.memset(table_load[:], 0.0)
            for i in range(2):
                g.memset(top2[i][:], -3.0e38)
                g.memset(gates[i][:, :, E:E + 1], 1.0)
            g.memset(ln_eps[:], LN_EPS)
            g.memset(rms_eps[:], RMS_EPS)
            g.memset(one_over_d[:], 1.0 / D).then_inc(consts_ready, 1)
            pool.wait_ge(consts_ready, 2)

            def inverse_std(v, i, lag):
                pool.wait_ge(stats_ready[i], v.at(lag, 1, 1))
                settled(pool, g.tensor_tensor(var_eps[i][:], mv[i][:, :, 1], ln_eps[:], ALU.add))
                g.tensor_tensor(std_inv[i][:], var_eps[i][:], minus_half[:], ALU.pow).then_inc(std_ready[i], 1)

            def split_up_weights(group, *weights):
                pool.wait_ge(loaded[group], n_loads[group])
                for whole, (w_hi, _) in weights:
                    g.tensor_copy(w_hi[:], whole)
                pool.drain()
                for whole, (w_hi, w_lo) in weights:
                    ins = g.tensor_tensor(w_lo[:], whole, w_hi[:].bitcast(F32), ALU.subtract)
                ins.then_inc(up_split, 1)

            def rms(v):
                pool.wait_ge(sq_ready, v.at(-1, 1, 1))
                settled(pool, g.tensor_tensor(mean_sq[:], sum_sq[:], one_over_d[:], ALU.mult))
                settled(pool, g.tensor_tensor(mean_sq[:], mean_sq[:], rms_eps[:], ALU.add))
                g.tensor_tensor(rms_inv[:], mean_sq[:], minus_half[:], ALU.pow).then_inc(rms_ready, 1)

            def plus(v):
                wait_weights(pool, v, 1)
                pool.wait_ge(x_loaded, v.at(-1, 16, 16))
                if v.a:
                    pool.wait_ge(*v.drain("OUT"))
                g.tensor_tensor(x_plus[:], x_row[:], b_out[:, 0:1, :].broadcast_to([P, NT, D]), ALU.add).then_inc(xplus_ready, 1)

            def head_product(v):
                for t, i in ((0, 1), (1, 0), (1, 1))[0 if v.a else 1:]:
                    if (t, i) != (1, 1):
                        pool.wait_ge(*v.drain(f"LQ{t}"))
                    q, k = head_pairs(t, half(i))
                    settled(pool, g.tensor_tensor(prod[:, t, half(i)], q, k, ALU.mult))
                    ins = add_pairs(prod[:, t, half(i)], DH1)
                    if i == 1:
                        ins.then_inc(prod_ready, 1)

            def add_pairs(x, n):
                return g.tensor_tensor(x[:, :, :, 0:n // 2], x[:, :, :, 0:n // 2], x[:, :, :, n // 2:n], ALU.add)

            def value_product(v, t, halves=(0, 1)):
                pool.wait_ge(exp1_ready, v.at(1, NT, t + 1))
                for i in halves:
                    ins = g.tensor_tensor(pv1[:, t, half(i)], *weights_and_values(t, i), ALU.mult)
                    if t == 0:
                        pool.drain()
                    ins = add_pairs(pv1[:, t, half(i)], NH1) if t == 0 else ins
                    ins.then_inc(pv1_ready, 1)

            def body(v):
                if v.it == 0:
                    split_up_weights(2, (router0_in_sb[:], router0), (up0_loaded, up0))
                if v.next:
                    rms(v)
                if v.it == 0:
                    split_up_weights(4, (up1_loaded, up1))
                if v.b:
                    wait_weights(pool, v, 3)
                    inverse_std(v, 1, 1)
                    pool.wait_ge(ln_ready[1], v.at(1, 1, 1))
                    g.tensor_tensor(x3[:], x2[:], bproj[:, 0:1, :].broadcast_to([P, NT, D]), ALU.add).then_inc(x2plus_ready, 1)
                    head_product(v)
                    if v.a:
                        value_product(v, 0)
                    value_product(v, 1, (0,))
                if v.a:
                    inverse_std(v, 0, 0)
                if v.b:
                    value_product(v, 1, (1,))
                if v.c:
                    inverse_std(v, 3, 2)
                if v.b:
                    inverse_std(v, 2, 1)
                if v.next:
                    plus(v)

            def before(v):
                rms(v)
                plus(v)

            run(pool, body, before)

        @block.scalar
        def _(act):
            sc = nc.scalar
            def squares_of(v):
                act.wait_ge(x_loaded, v.at(-1, 16, 16))
                for t in range(NT):
                    ins = sc.activation(h_row[:, t, :], x_row[:, t, :], ACT.Square, accum_out=sum_sq[:, t:t + 1])
                ins.then_inc(sq_ready, 1)

            def copy_out(v, name, dst, src):
                act.wait_ge(*v.fill(name))
                sc.activation(dst, src, ACT.Copy).then_inc(v.drain(name)[0], 1)

            def v_out(v, n):
                t, half = n // 2, n % 2
                copy_out(v, f"V{n}", values[:, t, half * 512:half * 512 + 512], v.bank(f"V{n}")[:, :])

            def o_out(v, s):
                copy_out(v, f"O{s}", oT[:, s, :], v.bank(f"O{s}")[:, 0:S])

            def qk_out(v, s):
                act.wait_ge(*v.fill(f"QK{s}"))
                sc.activation(qk_hi[:, s % 2], v.bank(f"QK{s}")[:, :].rearrange("p (a n) -> p a n", a=2), ACT.Copy).then_inc(qk_rounded, 1)

            def softmax_exp(v, h):
                unit = v.previous() if h < 2 else v
                act.wait_ge(max_ready, v.at(0, H, h + 1))
                for t in range(NT):
                    ins = sc.activation(probs[:, h // 2 % 2, h % 2, t, :], unit.bank(f"S{h}")[:, t * S:(t + 1) * S], ACT.Exp,
                                        bias=neg_max[:, h, t:t + 1],
                                        accum_out=row_sum[:, h // 2 % 2, h % 2 * NT + t:h % 2 * NT + t + 1])
                ins.then_inc(unit.drain(f"S{h}")[0], 1)

            def probsT_out(v, h):
                copy_out(v, f"T{h}", probsT[:, h % 2], v.bank(f"T{h}")[:, :].rearrange("p (k q) -> p k q", k=NT))

            def router_exp(v, i):
                lag = i + 1
                act.wait_ge(shifted_ready[i], v.at(lag, 1, 1))
                sc.activation(rexp[i][:], shifted[i][:], ACT.Exp).then_inc(rexp_ready[i], 1)

            def head_exp(v, t):
                act.wait_ge(score_ready, v.at(1, NT, t + 1))
                sc.activation(score1[:, t], score1[:, t], ACT.Exp, scale=1.0 / 8.0).then_inc(exp1_ready, 1)

            def gelu0(v, u):
                act.wait_ge(*v.fill(f"U0_{u}"))
                for m in range(M0):
                    ins = sc.activation(hid0[:, u, m, :], v.bank(f"U0_{u}")[:, m * S:(m + 1) * S], ACT.Gelu,
                                        bias=up0_b[:, u, m:m + 1])
                ins.then_inc(v.drain(f"U0_{u}")[0], 1)

            def gelu1(v, u):
                act.wait_ge(*v.fill(f"U1_{u}"))
                e, m = u // 2, u % 2 * 2
                sc.activation(hid1[:, e, m:m + 2, :], v.bank(f"U1_{u}")[:, :].rearrange("p (m n) -> p m n", m=2),
                              ACT.Gelu).then_inc(v.drain(f"U1_{u}")[0], 1)

            def transposed_probs(v, s):
                probsT_out(v, 2 * s)
                probsT_out(v, 2 * s + 1)

            def body(v):
                if v.b:
                    router_exp(v, 0)
                if v.a:
                    softmax_exp(v, 0)
                    softmax_exp(v, 1)
                    qk_out(v, 2)
                if v.c:
                    router_exp(v, 1)
                for s in range(HP):
                    if v.a and s == HP - 2:
                        o_out(v, s - 1)
                        transposed_probs(v, s)
                    if v.a and s + 1 < HP:
                        softmax_exp(v, 2 * s + 2)
                    if v.b and s == 3:
                        copy_out(v, "X2T", x2T[:], v.bank("X2T")[:, 0:S])
                    if v.a and s + 1 < HP:
                        softmax_exp(v, 2 * s + 3)
                    if v.a and s >= 1 and s != HP - 2:
                        o_out(v, s - 1)
                    if v.b and s == 1:
                        copy_out(v, "WT0", gates0T, v.bank("WT0")[0:E + 1, 0:S])
                    if v.a and s != HP - 2:
                        transposed_probs(v, s)
                    if v.a and s + 3 < HP:
                        qk_out(v, s + 3)
                    if v.b and s == 3:
                        for t in range(NT):
                            copy_out(v, f"LQ{t}", qkv1[:, t].rearrange("p h c d -> p (h c d)"), v.bank(f"LQ{t}")[:, 0:3 * D])
                    if v.next and s == 1:
                        squares_of(v)
                    if v.b and s == 5:
                        head_exp(v, 0)
                if v.b:
                    head_exp(v, 1)
                if v.a:
                    o_out(v, HP - 1)
                sc.activation(table_load[:], table_load[:], ACT.Gelu)
                if v.next:
                    for n in range(3):
                        v_out(v, n)
                if v.a:
                    for u in range(E + 1):
                        if v.b and u in (0, E // NT):
                            act.wait_ge(ao_ready, v.at(1, NT, u // (E // NT) + 1))
                        gelu0(v, u)
                if v.next:
                    v_out(v, 3)
                if v.b:
                    for u in range(2 * E):
                        gelu1(v, u)

            def before(v):
                squares_of(v)
                act.wait_ge(consts_ready, 2)
                for group, w, (w_hi, _), scale in zip((0, 1, 1), projections, (wv, wq, wk), (1.0, SCALE, 1.0)):
                    act.wait_ge(loaded[group], n_loads[group])
                    sc.activation(w_hi[:], w, ACT.Copy, scale=scale).then_inc(weights_rounded, 1)
                for n in range(4):
                    v_out(v, n)

            run(act, body, before)

        @block.vector
        def _(dve):
            ve = nc.vector
            dve.wait_ge(stored, 16)
            dve.wait_ge(consts_ready, 2)

            def head_max(v, h):
                dve.wait_ge(*v.fill(f"S{h}"))
                ve.tensor_reduce(neg_max[:, h, :], v.bank(f"S{h}")[:, :].rearrange("p (t k) -> p t k", t=NT),
                                 AX.X, ALU.max, negate=True).then_inc(max_ready, 1)

            def normalise(v, s):
                unit = v.previous() if s == 0 else v
                for j in range(2):
                    dve.wait_ge(*unit.drain(f"S{2 * s + j}"))
                settled(dve, ve.reciprocal(row_inv[:, s % 2, :], row_sum[:, s % 2, :]))
                for j in range(2):
                    for t in range(NT):
                        n = j * NT + t
                        ins = ve.tensor_scalar(probs[:, s % 2, j, t, :], probs[:, s % 2, j, t, :], row_inv[:, s % 2, n:n + 1],
                                               None, ALU.mult)
                    ins.then_inc(probs_ready, 1)

            def lower_qk(v, s):
                if s >= 2:
                    dve.wait_ge(qk_rounded, v.at(0, HP - 2, s - 1))
                ve.tensor_tensor(qk_lo[:, s % 2], v.bank(f"QK{s}")[:, :].rearrange("p (a n) -> p a n", a=2),
                                 qk_hi[:, s % 2].bitcast(F32), ALU.subtract).then_inc(v.drain(f"QK{s}")[0], 1)

            def split_weights(n):
                (w_hi, w_lo), scale = (wv, wq, wk)[n], (1.0, SCALE, 1.0)[n]
                dve.wait_ge(weights_rounded, n + 1)
                ve.scalar_tensor_tensor(w_lo[:], projections[n], scale, w_hi[:].bitcast(F32), ALU.mult, ALU.subtract).then_inc(weights_split, 1)

            def first_pair(v, s):
                dve.wait_ge(*v.fill(f"QK{s}"))
                settled(dve, ve.tensor_copy(qk_hi[:, s], v.bank(f"QK{s}")[:, :].rearrange("p (a n) -> p a n", a=2)))
                lower_qk(v, s)

            def ln_stats(v, i, y):
                for t in range(NT):
                    settled(dve, ve.bn_stats(stats[i][:, t, :], y[:, t, :]))
                for t in range(NT):
                    ins = ve.bn_aggr(mv[i][:, t, :], stats[i][:, t, :])
                ins.then_inc(stats_ready[i], 1)

            def ln_apply(v, i, x, lag):
                dve.wait_ge(std_ready[i], v.at(lag, 1, 1))
                for t in range(NT):
                    ins = ve.tensor_scalar(x[:, t, :], x[:, t, :], mv[i][:, t, 0:1], std_inv[i][:, t:t + 1],
                                           ALU.subtract, ALU.mult)
                ins.then_inc(ln_ready[i], 1)

            def route(v, i):
                for t in range(NT):
                    settled(dve, ve.max(top8[i][:, t, :], logits[i][:, t, :]))
                settled(dve, ve.tensor_copy(top2[i][:, :, 0:2], top8[i][:, :, 0:2]))
                for t in range(NT):
                    settled(dve, ve.match_replace(marked[i][:, t, :], top2[i][:, t, :], logits[i][:, t, :], -3.0e38))
                ve.tensor_tensor(shifted[i][:], logits[i][:], top8[i][:, :, 0:1].broadcast_to([P, NT, E]),
                                 ALU.subtract).then_inc(shifted_ready[i], 1)
                settled(dve, ve.tensor_tensor(marked[i][:], marked[i][:], logits[i][:], ALU.not_equal))

            def gate(v, i, lag):
                dve.wait_ge(rexp_ready[i], v.at(lag, 1, 1))
                settled(dve, ve.reduce_sum(rsum[i][:], rexp[i][:], AX.X))
                settled(dve, ve.reciprocal(rsum[i][:], rsum[i][:]))
                settled(dve, ve.tensor_tensor(marked[i][:], marked[i][:], rexp[i][:], ALU.mult))
                ins = ve.tensor_tensor(gates[i][:, :, 0:E], marked[i][:], rsum[i][:].rearrange("p (t a) -> p t a", a=1).broadcast_to([P, NT, E]),
                                       ALU.mult)
                if i == 0:
                    ins.then_inc(gates_ready, 1)
                settled(dve, ins)

            def mix(v, name, i, experts, acc, first, drain=True):
                dve.wait_ge(*v.fill(name))
                y = v.bank(name)[:, 0:len(experts) * NT * D].rearrange("p (j t d) -> p j t d", j=len(experts), t=NT)
                for j, e in enumerate(experts):
                    src = first if e == 0 else acc
                    for t in range(NT):
                        ins = ve.scalar_tensor_tensor(acc[:, t, :], y[:, j, t, :], gates[i][:, t, e:e + 1], src[:, t, :],
                                                      ALU.mult, ALU.add)
                    if e == experts[-1]:
                        ins.then_inc(v.drain(name)[0], 1)
                    if e != experts[-1] or drain:
                        settled(dve, ins)

            def head_product(v):
                dve.wait_ge(*v.drain("LQ0"))
                for i in range(1 if v.a else 2):
                    q, k = head_pairs(0, half(i))
                    ins = ve.tensor_tensor(prod[:, 0, half(i)], q, k, ALU.mult)
                    if i == 1:
                        ins.then_inc(prod_ready, 1)
                    settled(dve, ins)

            def value_product(v):
                for i in range(2):
                    ins = ve.tensor_tensor(pv1[:, 0, half(i)], *weights_and_values(0, i), ALU.mult)
                    ins.then_inc(pv1_ready, 1)
                    settled(dve, ins)

            def head_sum(v, t, i):
                if (t, i) != (0, 0):
                    dve.wait_ge(prod_ready, v.at(1, NT, t + 1))
                own = t == 0 and (i == 0 or not v.a)
                n = DH1 if own else DH1 // 2
                settled(dve, ve.reduce_sum(score1[:, t, half(i)], prod[:, t, half(i), :, 0:n], AX.X))

            def head_shift(v, t):
                settled(dve, ve.reduce_max(max1[:], score1[:, t], AX.X))
                ve.tensor_tensor(score1[:, t], score1[:, t], max1[:].rearrange("p (h a) -> p h a", a=1).broadcast_to([P, NH1, NH1]),
                                 ALU.subtract).then_inc(score_ready, 1)

            def head_softmax_sum(v, t):
                dve.wait_ge(exp1_ready, v.at(1, NT, t + 1))
                settled(dve, ve.reduce_sum(sum1[:, t], score1[:, t], AX.X))
                settled(dve, ve.reciprocal(inv1[:, t], sum1[:, t]))

            def head_mix(v, t, i):
                dve.wait_ge(pv1_ready, v.at(1, 2 * NT, 2 * t + i + 1))
                n = NH1 // 2 if v.a and t == 0 else NH1
                settled(dve, ve.reduce_sum(ao[:, t, half(i)], pv1[:, t, half(i), :, 0:n], AX.X))

            def head_divide(v, t):
                ve.tensor_tensor(ao[:, t], ao[:, t], inv1[:, t].rearrange("p (h a) -> p h a", a=1).broadcast_to([P, NH1, DH1]),
                                 ALU.mult).then_inc(ao_ready, 1)

            def input_norm(v):
                dve.wait_ge(rms_ready, v.at(-1, 1, 1))
                dve.wait_ge(x_loaded, v.at(-1, 16, 16))
                for t in range(NT):
                    ins = ve.tensor_scalar(h_row[:, t, :], x_row[:, t, :], rms_inv[:, t:t + 1], None, ALU.mult)
                ins.then_inc(h_ready, 1)

            def input_transposed(v):
                dve.wait_ge(*v.fill("HT"))
                settled(dve, ve.tensor_scalar(hT[0][:], v.bank("HT")[:, 0:S], nscale[:, 0:1], None, ALU.mult))
                ve.scalar_tensor_tensor(hT[1][:], v.bank("HT")[:, 0:S], nscale[:, 0:1], hT[0][:].bitcast(F32),
                                        ALU.mult, ALU.subtract).then_inc(v.drain("HT")[0], 1)

            def residual(v, name, y, x):
                dve.wait_ge(*v.fill(name))
                ve.tensor_tensor(y[:], v.bank(name)[:, 0:NT * D].rearrange("p (t d) -> p t d", t=NT),
                                 x[:], ALU.add).then_inc(v.drain(name)[0], 1)
                dve.drain()

            def transposed_out(v, name, xT=None, halves=None):
                dve.wait_ge(*v.fill(name))
                source = v.bank(name)[:, 0:S]
                if halves:
                    ins = ve.tensor_copy(halves[0][:], source)
                if xT:
                    ins = ve.tensor_copy(xT[:], source)
                if halves:
                    settled(dve, ins)
                    ins = ve.tensor_tensor(halves[1][:], source, halves[0][:].bitcast(F32), ALU.subtract)
                ins.then_inc(v.drain(name)[0], 1)

            def fill_out(v, s, place):
                for name in fill_units(v.it, s, place):
                    if name[:3] == "D0p":
                        p = int(name[3:])
                        mix(v, name, 0, (2 * p, 2 * p + 1), x2, x1, not v.a or p == 3)
                    if name == "D0base":
                        residual(v, name, x2, x2)
                        ln_stats(v, 1, x2)
                    if name[:3] == "D1e":
                        mix(v, name, 1, (int(name[3:]),), x4, x3, not v.a or s >= HP - 2)

            def body(v):
                if v.b:
                    gate(v, 0, 1)
                    mix(v, "D0p0", 0, (0, 1), x2, x1, not v.a)
                if v.a:
                    normalise(v, 0)
                for s in range(HP):
                    if v.b and s == 3:
                        ln_apply(v, 1, x2, 1)
                    if v.a and s + 1 < HP:
                        head_max(v, 2 * s + 2)
                        head_max(v, 2 * s + 3)
                    if v.a and s + 2 < HP:
                        lower_qk(v, s + 2)
                    if v.b and s == 0:
                        mix(v, "D0p1", 0, (2, 3), x2, x1, not v.a)
                    if s not in (0, 3, HP - 1):
                        fill_out(v, s - 1, 1)
                    fill_out(v, s, 0)
                    if v.a and s + 1 < HP:
                        normalise(v, s + 1)
                    if v.c and s == 1:
                        gate(v, 1, 2)
                        dve.wait_ge(stored, v.at(2, 16, 16))
                    if s in (2, HP - 2):
                        fill_out(v, s, 1)
                    if v.next and s == 3:
                        input_norm(v)
                    if v.next and s == HP - 2:
                        input_transposed(v)
                    if v.b and s == 4:
                        head_product(v)
                    if v.b and s in (5, 6):
                        head_sum(v, s - 5, 0)
                        head_sum(v, s - 5, 1)
                        head_shift(v, s - 5)
                if v.b:
                    head_softmax_sum(v, 0)
                    if not v.a:
                        value_product(v)
                fill_out(v, HP - 1, 1)
                if v.b:
                    head_mix(v, 0, 0)
                if v.a:
                    dve.wait_ge(xplus_ready, v.at(0, 1, 1))
                    residual(v, "OUT", x1, x_plus)
                    ln_stats(v, 0, x1)
                if v.b:
                    head_mix(v, 0, 1)
                    head_divide(v, 0)
                if v.c:
                    mix(v, "D1e6", 1, (6,), x4, x3)
                if v.a:
                    ln_apply(v, 0, x1, 0)
                if v.b:
                    head_softmax_sum(v, 1)
                if v.a:
                    transposed_out(v, "X1T", halves=x1T)
                if v.c:
                    mix(v, "D1e7", 1, (7,), x4, x3)
                if v.b:
                    head_mix(v, 1, 0)
                    head_mix(v, 1, 1)
                    head_divide(v, 1)
                if v.b:
                    transposed_out(v, "AOT", aoT)
                if v.c:
                    ln_stats(v, 3, x4)
                if v.b:
                    dve.wait_ge(x2plus_ready, v.at(1, 1, 1))
                    residual(v, "PROJ", x3, x3)
                    ln_stats(v, 2, x3)
                if v.a:
                    dve.wait_ge(*v.fill("R0"))
                    ve.tensor_tensor(logits[0][:], v.bank("R0")[:, 0:NT * E].rearrange("p (t e) -> p t e", t=NT),
                                     router0_b[:, 0:1, :].broadcast_to([P, NT, E]), ALU.add).then_inc(v.drain("R0")[0], 1)
                    dve.drain()
                if v.c:
                    ln_apply(v, 3, x4, 2)
                if v.b:
                    ln_apply(v, 2, x3, 1)
                    transposed_out(v, "X3T", x3T, x3T_parts)
                if v.next:
                    first_pair(v, 0)
                if v.a:
                    route(v, 0)
                if v.b:
                    dve.wait_ge(*v.fill("R1"))
                    ve.tensor_copy(logits[1][:], v.bank("R1")[:, 0:NT * E].rearrange("p (t e) -> p t e", t=NT)).then_inc(v.drain("R1")[0], 1)
                    dve.drain()
                    route(v, 1)
                if v.next:
                    first_pair(v, 1)
                    head_max(v, 0)
                    head_max(v, 1)

            def before(v):
                input_norm(v)
                split_weights(0)
                input_transposed(v)
                split_weights(1)
                split_weights(2)
                first_pair(v, 0)
                first_pair(v, 1)
                head_max(v, 0)
                head_max(v, 1)

            run(dve, body, before)

        @block.tensor
        def _(pe):
            te = nc.tensor
            pe.wait_ge(consts_ready, 2)

            def tokens(t):
                return slice(t * P, (t + 1) * P)

            def transpose_row(bank, src):
                for t in range(NT):
                    ins = te.transpose(bank[0:src.shape[2], tokens(t)], src[:, t, :], ident[:])
                return ins

            def wait_drained(v, name, source):
                if v.nth[source][0] != v.nth[name][0]:
                    pe.wait_ge(*v.drain(source))

            def parts(pair, columns):
                return pair[0][:, columns], pair[1][:, columns]

            def products(out, stationary, moving):
                (s_hi, s_lo), (m_hi, m_lo) = stationary, moving
                te.matmul(out, s_lo, m_hi, start=True, stop=False)
                te.matmul(out, s_hi, m_lo, start=False, stop=False)
                return te.matmul(out, s_hi, m_hi, start=False, stop=True)

            def unit(v, name):
                bank = v.bank(name)

                if name[0] == "V":
                    n = int(name[1:])
                    if n == 0:
                        if v.it < 0:
                            pe.wait_ge(weights_split, 1)
                        wait_drained(v, name, "HT")
                    t, half = tokens(n // 2), slice(n % 2 * 512, n % 2 * 512 + 512)
                    return products(bank[:, :], parts(hT, t), parts(wv, half))
                if name[:2] == "QK":
                    s = int(name[2:])
                    if s == 0:
                        if v.it < 0:
                            pe.wait_ge(weights_split, 3)
                    for n, w in enumerate((wq, wk)):
                        ins = products(bank[:, n * S:(n + 1) * S], parts(w, tokens(s)), parts(hT, slice(0, S)))
                    return ins
                if name[0] == "S":
                    h = int(name[1:])
                    s, r = h // 2, slice(h % 2 * DH, h % 2 * DH + DH)
                    if s == 1:
                        pe.wait_ge(*v.previous().drain("QK1"))
                    else:
                        wait_drained(v, name, f"QK{s}")
                    for t in range(NT):
                        ins = products(bank[:, t * S:(t + 1) * S], (qk_hi[r, s % 2, 0, tokens(t)], qk_lo[r, s % 2, 0, tokens(t)]),
                                       (qk_hi[r, s % 2, 1, :], qk_lo[r, s % 2, 1, :]))
                    return ins
                if name[0] == "T":
                    h = int(name[1:])
                    pe.wait_ge(probs_ready, v.at(0, H, h + 1))
                    for k in range(NT):
                        for t in range(NT):
                            ins = te.transpose(bank[:, k * S + t * P:k * S + (t + 1) * P], probs[:, h // 2 % 2, h % 2, t, tokens(k)], ident[:])
                    return ins
                if name == "OUT":
                    wait_weights(pe, v, 2)
                if name == "D0p0":
                    wait_weights(pe, v, 3)
                if name == "X3T":
                    wait_weights(pe, v, 4)
                if name == "OUT":
                    for t in range(NT):
                        for s in range(HP):
                            if t == 0 and s == HP - 1:
                                wait_drained(v, name, f"O{s}")
                            ins = te.matmul(bank[:, tokens(t)], oT[:, s, tokens(t)], wo[:, s, :], start=s == 0, stop=s == HP - 1)
                    return ins
                if name[0] == "O":
                    s = int(name[1:])
                    for j in range(2):
                        pe.wait_ge(*v.drain(f"T{2 * s + j}"))
                    for k in range(NT):
                        for j in range(2):
                            r = slice(j * DH, j * DH + DH)
                            ins = te.matmul(bank[r, 0:S], values[:, k, s * P + j * DH:s * P + j * DH + DH],
                                            probsT[:, j, k, :], start=k == 0, stop=k == NT - 1)
                    return ins
                if name == "X1T":
                    pe.wait_ge(ln_ready[0], v.at(0, 1, 1))
                    return transpose_row(bank, x1)
                if name == "X2T":
                    pe.wait_ge(ln_ready[1], v.at(1, 1, 1))
                    return transpose_row(bank, x2)
                if name == "X3T":
                    pe.wait_ge(ln_ready[2], v.at(1, 1, 1))
                    return transpose_row(bank, x3)
                if name == "HT":
                    pe.wait_ge(h_ready, v.at(-1, 1, 1))
                    return transpose_row(bank, h_row)
                if name in ("R0", "R1"):
                    for t in range(NT):
                        out = bank[:, t * E:(t + 1) * E]
                        if name == "R0":
                            ins = products(out, parts(x1T, tokens(t)), parts(router0, slice(0, E)))
                        else:
                            ins = te.matmul(out, x3T[:, tokens(t)], router1[:], start=True, stop=True)
                    return ins
                if name == "WT0":
                    pe.wait_ge(gates_ready, v.at(1, 1, 1))
                    return transpose_row(bank, gates[0])
                if name[:3] == "U0_":
                    e = int(name[3:])
                    if e == 0:
                        wait_drained(v, name, "X1T")
                        if v.it == 0:
                            pe.wait_ge(up_split, 1)
                    for m in range(M0):
                        ins = products(bank[:, m * S:(m + 1) * S], (up0[0][:, e, tokens(m)], up0[1][:, e, tokens(m)]), parts(x1T, slice(0, S)))
                    return ins
                if name[:3] == "U1_":
                    u = int(name[3:])
                    if u == 0:
                        wait_drained(v, name, "X3T")
                        if v.it == 1:
                            pe.wait_ge(up_split, 2)
                    for m in range(2):
                        out, columns = bank[:, m * S:(m + 1) * S], tokens(u % 2 * 2 + m)
                        if u // 2 < SPLIT1:
                            ins = products(out, (up1[0][:, u // 2, columns], up1[1][:, u // 2, columns]), parts(x3T_parts, slice(0, S)))
                        else:
                            ins = te.matmul(out, up1_whole[:, u // 2 - SPLIT1, columns], x3T[:], start=True, stop=True)
                    return ins
                if name == "D0base":
                    wait_drained(v, name, "WT0")
                    for t in range(NT):
                        for k in range(M0):
                            te.matmul(bank[:, tokens(t)], hid0[:, E, k, tokens(t)], down0[:, E, k, :], start=k == 0, stop=False)
                        ins = te.matmul(bank[:, tokens(t)], gates0T[:, tokens(t)], down0_b[:], start=False, stop=True)
                    return ins
                if name[:3] in ("D0p", "D1e"):
                    hid, down, m, n = ((hid0, down0, M0, 2), (hid1, down1, M1, 1))[int(name[1])]
                    for j in range(n):
                        e = n * int(name[3:]) + j
                        for t in range(NT):
                            for k in range(m):
                                ins = te.matmul(bank[:, (j * NT + t) * P:(j * NT + t + 1) * P], hid[:, e, k, tokens(t)],
                                                down[:, e, k, :], start=k == 0, stop=k == m - 1)
                    return ins
                if name in ("LQ0", "LQ1"):
                    t = int(name[2])
                    wait_drained(v, name, "X2T")
                    return te.matmul(bank[:, 0:3 * D], x2T[:, tokens(t)], wqkv1[:], start=True, stop=True)
                if name == "AOT":
                    pe.wait_ge(ao_ready, v.at(1, NT, NT))
                    return transpose_row(bank, ao[:].rearrange("p t h d -> p t (h d)"))
                assert name == "PROJ"
                wait_drained(v, name, "AOT")
                for t in range(NT):
                    ins = te.matmul(bank[:, tokens(t)], aoT[:, tokens(t)], wproj[:], start=True, stop=True)
                return ins

            def body(v):
                for name, bank in (pe_units(v.it) if v.it >= 0 else PRE):
                    free, count = v.drain(name, before=1)
                    if v.it > 0 or count:
                        pe.wait_ge(free, count)
                    unit(v, name).then_inc(v.fill(name)[0], 1)

            run(pe, body, body)


def kernel(**inputs):
    import numpy as np
    import concourse.bacc as bacc
    from concourse import mybir as mb
    from concourse.bass_utils import run_bass_kernel_spmd

    i = {k: np.asarray(v) for k, v in inputs.items()}
    E_, H0, H1 = 8, 256, 512
    arrays = {
        "x": i["L0_attn_x"], "norm_scale": i["L0_attn_norm_scale"], "wq": i["L0_attn_wq"], "wk": i["L0_attn_wk"],
        "wv": i["L0_attn_wv"], "wo": i["L0_attn_w_out"], "b_out": i["L0_attn_b_out"],
        "router0": i["L0_ffn_router_w"], "router0_b": i["L0_ffn_router_b"], "sw1": i["L0_ffn_sw1"],
        "sb1": i["L0_ffn_sb1"].reshape(H0 // 128, 128).transpose(1, 0), "sw2": i["L0_ffn_sw2"], "sb2": i["L0_ffn_sb2"],
        "rw1": i["L0_ffn_rw1"], "rb1": i["L0_ffn_rb1"].reshape(E_, H0 // 128, 128).transpose(2, 0, 1),
        "rw2": i["L0_ffn_rw2"], "rb2": i["L0_ffn_rb2"],
        "wqkv1": i["L1_attn_Wqkv"].transpose(1, 0), "wproj": i["L1_attn_Wproj"].transpose(1, 0), "bproj": i["L1_attn_bproj"],
        "router1": i["L1_ffn_router_w"].transpose(1, 0), "w1": i["L1_ffn_w1"].transpose(2, 0, 1),
        "w2": i["L1_ffn_w2"].reshape(E_, 128, H1 // 128, 128).transpose(3, 0, 2, 1),
    }
    arrays = {f"in_{k}": np.ascontiguousarray(v) for k, v in arrays.items()}
    nc = bacc.Bacc("TRN2", target_bir_lowering=False, num_devices=1)
    args = [nc.dram_tensor(k, v.shape, mb.dt.from_np(v.dtype), kind="ExternalInput").ap() for k, v in arrays.items()]
    out = nc.dram_tensor("out", (16, 256, 128), mb.dt.from_np(np.dtype("float32")), kind="ExternalOutput").ap()
    transformer_blocks(nc, *args, out)
    r = run_bass_kernel_spmd(nc, [arrays], core_ids=[0])
    return r.results[0]["out"]
```
